# Optimizing a Trainium2 kernel written in Bass

```python
import numpy as np
import jax
import jax.numpy as jnp

def _softmax(x, axis=-1):
    return jax.nn.softmax(x, axis=axis)

def _gelu(x):
    return jax.nn.gelu(x, approximate=True)

def _silu(x):
    return jax.nn.silu(x)

def _sigmoid(x):
    return jax.nn.sigmoid(x)

def _layernorm(x, axis=-1, eps=1e-05):
    m = jnp.mean(x, axis=axis, keepdims=True)
    v = jnp.var(x, axis=axis, keepdims=True)
    return (x - m) / jnp.sqrt(v + eps)

def _scatter_add(tgt, idx, src, axis=0):
    return tgt.at[idx].add(src)

def _segment_sum(src, seg, n):
    return jax.ops.segment_sum(src, seg, n)
kernel_name = 'mk_flamingo_gated_d2_seqx_r8_2d81a1'

def setup_inputs(seed: int=0):
    np.random.seed(seed)
    _w = jnp.asarray

    def _rec_inputs():
        import jax
        import jax.numpy as jnp
        _rk = jax.random.key(seed)
        x = 7.22e-05 + 1 * jax.random.normal(jax.random.fold_in(_rk, 1), (8, 256, 128), jnp.float32)
        _lenS = 256 - jax.random.randint(jax.random.fold_in(_rk, 7), (8,), 0, max(1, 256 // 4) + 1, jnp.int32)
        _lenS2 = 256 - jax.random.randint(jax.random.fold_in(_rk, 8), (8,), 0, max(1, 256 // 4) + 1, jnp.int32)
        _ctx_1024P = jax.random.normal(jax.random.fold_in(_rk, 11), (8, 16, 128), jnp.float32)
        _ctx_1024c = jax.random.dirichlet(jax.random.fold_in(_rk, 511), 0.3 * jnp.ones((16,), jnp.float32), (8, 256))
        _ctx_1024t = jnp.einsum('bsk,bkd->bsd', _ctx_1024c, _ctx_1024P)
        _ctx_1024t = _ctx_1024t * jax.lax.rsqrt(jnp.mean(jnp.square(_ctx_1024t)) + 1e-12) * 0.953939
        ctx_1024 = 4.13588e-05 + 0.999923 * (_ctx_1024t + 0.3 * jax.random.normal(jax.random.fold_in(_rk, 611), (8, 256, 128), jnp.float32))
        fside_BxS2_0 = 0.0132156 + 1.00766 * jax.random.normal(jax.random.fold_in(_rk, 12), (8, 256), jnp.float32)
        _validS = jnp.arange(256)[None, :] < _lenS[:, None]
        _validS2 = jnp.arange(256)[None, :] < _lenS2[:, None]
        _causal = jnp.tril(jnp.ones((256, 256), dtype=bool))
        mask_BxS2_bk0 = jnp.logical_not(jnp.broadcast_to(_validS2[:, :], (8, 256)))
        _g = jax.random.normal(jax.random.fold_in(_rk, 9001), (2, 2), jnp.float32)
        _g = jnp.sign(_g) * jnp.maximum(jnp.abs(_g), 1.0) + (_g == 0) * 1.0
        g_xattn = _g[0]
        g_ffn = _g[1]
        return (x, ctx_1024, fside_BxS2_0, mask_BxS2_bk0, g_xattn, g_ffn)
    x, ctx_1024, fside_BxS2_0, mask_BxS2_bk0, g_xattn, g_ffn = _rec_inputs()

    def _L0_xattn_setup():
        import jax, jax.numpy as jnp
        import numpy as np
        NUM_HEADS = 16

        def trinity_mask(txt_tok, img_tok):
            assert img_tok % 3 == 0, 'Invalid text token sizes'
            sit = img_tok // 3
            N = txt_tok + img_tok
            i = jnp.arange(N)[:, None]
            j = jnp.arange(N)[None, :]
            img_img = (i < img_tok) & (j < img_tok) & (i // sit == j // sit)
            txt_img = (i >= img_tok) & (j < img_tok)
            txt_txt = (i >= img_tok) & (j >= img_tok) & (i >= j)
            return img_img | txt_img | txt_txt
        key = jax.random.key(seed)
        ks = jax.random.split(key, 12)
        B, TXT, IMG = (4, 64, 192)
        N = TXT + IMG
        DQ, DKV = (128, 128)
        s = lambda d: 1.0 / np.sqrt(d).astype(np.float32)
        return {'q': jax.random.normal(ks[0], (B, N, DQ), jnp.float32), 'kv': jax.random.normal(ks[1], (B, N, DKV), jnp.float32), 'Wq': jax.random.normal(ks[2], (DQ, DQ), jnp.float32) * s(DQ), 'bq': jnp.zeros((DQ,), jnp.float32), 'Wk': jax.random.normal(ks[3], (DKV, DQ), jnp.float32) * s(DKV), 'bk': jnp.zeros((DQ,), jnp.float32), 'Wv': jax.random.normal(ks[4], (DKV, DQ), jnp.float32) * s(DKV), 'bv': jnp.zeros((DQ,), jnp.float32), 'Wo': jax.random.normal(ks[5], (DQ, DQ), jnp.float32) * s(DQ), 'bo': jnp.zeros((DQ,), jnp.float32), 'txt_tok_len': TXT, 'img_tok_len': IMG}
    _L0_xattn_all = _L0_xattn_setup()
    _L0_xattn_in = {k: v for k, v in _L0_xattn_all.items() if k in ('Wq', 'bq', 'Wk', 'bk', 'Wv', 'bv', 'Wo', 'bo')}
    del _L0_xattn_all

    def _L0_ffn_setup():
        import jax, jax.numpy as jnp
        import numpy as np
        BLOCK_SIZE = 32
        FP6_E2M3_MAX = 7.5

        def _build_fp6_e2m3_grid():
            vals = set()
            for bits in range(64):
                s = bits >> 5 & 1
                e = bits >> 3 & 3
                m = bits & 7
                v = m / 8.0 if e == 0 else (1.0 + m / 8.0) * 2.0 ** (e - 1)
                vals.add(-v if s else v)
            return np.array(sorted(vals), dtype=np.float32)
        _GRID = jnp.asarray(_build_fp6_e2m3_grid())

        def _nearest_on_grid(x, grid):
            idx = jnp.clip(jnp.searchsorted(grid, x), 0, grid.shape[0] - 1)
            idx_lo = jnp.maximum(idx - 1, 0)
            v_hi = grid[idx]
            v_lo = grid[idx_lo]
            return jnp.where(jnp.abs(x - v_lo) <= jnp.abs(x - v_hi), v_lo, v_hi)

        def _mx_quantize(t, eps=1e-30):
            rows, K = t.shape
            blocks = t.reshape(rows, K // BLOCK_SIZE, BLOCK_SIZE)
            scales = jnp.maximum(jnp.max(jnp.abs(blocks), axis=-1) / FP6_E2M3_MAX, eps)
            q = _nearest_on_grid(blocks / scales[..., None], _GRID)
            return (q, scales)
        key = jax.random.key(seed)
        k1, k2, k3 = jax.random.split(key, 3)
        x = jax.random.normal(k1, (8, 1024, 128), dtype=jnp.float32)
        weight = jax.random.normal(k2, (128, 128), dtype=jnp.float32) * 0.02
        bias = jax.random.normal(k3, (128,), dtype=jnp.float32) * 0.02
        return {'x': x, 'weight': weight, 'bias': bias}
    _L0_ffn_all = _L0_ffn_setup()
    _L0_ffn_in = {k: v for k, v in _L0_ffn_all.items() if k in ('weight', 'bias')}
    del _L0_ffn_all

    def _L1_xattn_setup():
        import jax, jax.numpy as jnp
        import numpy as np
        EMBED_DIM = 128
        NUM_HEADS = 16
        HEAD_DIM = EMBED_DIM // NUM_HEADS
        B, SQ, SK = (2, 256, 256)
        key = jax.random.key(seed)
        ks = jax.random.split(key, 10)
        s = 1.0 / np.sqrt(EMBED_DIM)
        return {'tgt': jax.random.normal(ks[0], (B, SQ, EMBED_DIM), jnp.float32), 'mem': jax.random.normal(ks[1], (B, SK, EMBED_DIM), jnp.float32), 'attn_bias': jax.random.normal(ks[2], (B, SK), jnp.float32), 'memory_key_padding_mask': jax.random.randint(ks[3], (B, SK), 0, 2).astype(bool), 'Wq_w': jax.random.normal(ks[4], (EMBED_DIM, EMBED_DIM), jnp.float32) * s, 'Wq_b': jnp.zeros((EMBED_DIM,), jnp.float32), 'Wkv_w': jax.random.normal(ks[5], (2 * EMBED_DIM, EMBED_DIM), jnp.float32) * s, 'Wkv_b': jnp.zeros((2 * EMBED_DIM,), jnp.float32), 'out_w': jax.random.normal(ks[6], (EMBED_DIM, EMBED_DIM), jnp.float32) * s, 'out_b': jnp.zeros((EMBED_DIM,), jnp.float32)}
    _L1_xattn_all = _L1_xattn_setup()
    _L1_xattn_in = {k: v for k, v in _L1_xattn_all.items() if k in ('Wq_w', 'Wq_b', 'Wkv_w', 'Wkv_b', 'out_w', 'out_b')}
    del _L1_xattn_all

    def _L1_ffn_setup():
        import jax, jax.numpy as jnp
        import numpy as np
        B, S, D, F, E = (2, 256, 128, 512, 8)
        LN_EPS = 1e-05

        def _layer_norm(x, gamma, beta):
            mu = jnp.mean(x, axis=-1, keepdims=True)
            var = jnp.mean(jnp.square(x - mu), axis=-1, keepdims=True)
            return (x - mu) * jax.lax.rsqrt(var + LN_EPS) * gamma + beta
        key = jax.random.key(seed)
        ks = jax.random.split(key, 8)

        def xavier(k, shape):
            fan_in, fan_out = (shape[-1], shape[-2])
            a = jnp.sqrt(6.0 / (fan_in + fan_out))
            return jax.random.uniform(k, shape, jnp.float32, -a, a)
        return {'tgt': jax.random.normal(ks[0], (B, S, D), jnp.float32), 'Wr': xavier(ks[1], (E, D)), 'br': jnp.zeros((E,), jnp.float32), 'W1': xavier(ks[2], (E, F, D)), 'b1': jnp.zeros((E, F), jnp.float32), 'W2': xavier(ks[3], (E, D, F)), 'b2': jnp.zeros((E, D), jnp.float32), 'gamma': jnp.ones((D,), jnp.float32), 'beta': jnp.zeros((D,), jnp.float32)}
    _L1_ffn_all = _L1_ffn_setup()
    _L1_ffn_in = {k: v for k, v in _L1_ffn_all.items() if k in ('Wr', 'br', 'W1', 'b1', 'W2', 'b2', 'gamma', 'beta')}
    del _L1_ffn_all
    return {'x': x, 'ctx_1024': ctx_1024, 'fside_BxS2_0': fside_BxS2_0, 'mask_BxS2_bk0': mask_BxS2_bk0, 'g_xattn': g_xattn, 'g_ffn': g_ffn, 'L0_xattn_Wq': _L0_xattn_in['Wq'], 'L0_xattn_bq': _L0_xattn_in['bq'], 'L0_xattn_Wk': _L0_xattn_in['Wk'], 'L0_xattn_bk': _L0_xattn_in['bk'], 'L0_xattn_Wv': _L0_xattn_in['Wv'], 'L0_xattn_bv': _L0_xattn_in['bv'], 'L0_xattn_Wo': _L0_xattn_in['Wo'], 'L0_xattn_bo': _L0_xattn_in['bo'], 'L0_ffn_weight': _L0_ffn_in['weight'], 'L0_ffn_bias': _L0_ffn_in['bias'], 'L1_xattn_Wq_w': _L1_xattn_in['Wq_w'], 'L1_xattn_Wq_b': _L1_xattn_in['Wq_b'], 'L1_xattn_Wkv_w': _L1_xattn_in['Wkv_w'], 'L1_xattn_Wkv_b': _L1_xattn_in['Wkv_b'], 'L1_xattn_out_w': _L1_xattn_in['out_w'], 'L1_xattn_out_b': _L1_xattn_in['out_b'], 'L1_ffn_Wr': _L1_ffn_in['Wr'], 'L1_ffn_br': _L1_ffn_in['br'], 'L1_ffn_W1': _L1_ffn_in['W1'], 'L1_ffn_b1': _L1_ffn_in['b1'], 'L1_ffn_W2': _L1_ffn_in['W2'], 'L1_ffn_b2': _L1_ffn_in['b2'], 'L1_ffn_gamma': _L1_ffn_in['gamma'], 'L1_ffn_beta': _L1_ffn_in['beta']}

def reference(x, ctx_1024, fside_BxS2_0, mask_BxS2_bk0, g_xattn, g_ffn, L0_xattn_Wq, L0_xattn_bq, L0_xattn_Wk, L0_xattn_bk, L0_xattn_Wv, L0_xattn_bv, L0_xattn_Wo, L0_xattn_bo, L0_ffn_weight, L0_ffn_bias, L1_xattn_Wq_w, L1_xattn_Wq_b, L1_xattn_Wkv_w, L1_xattn_Wkv_b, L1_xattn_out_w, L1_xattn_out_b, L1_ffn_Wr, L1_ffn_br, L1_ffn_W1, L1_ffn_b1, L1_ffn_W2, L1_ffn_b2, L1_ffn_gamma, L1_ffn_beta):
    import jax
    import jax.numpy as jnp

    def _L0_xattn_ref(q, kv, Wq, bq, Wk, bk, Wv, bv, Wo, bo, txt_tok_len, img_tok_len):
        import jax, jax.numpy as jnp
        import numpy as np
        NUM_HEADS = 16

        def trinity_mask(txt_tok, img_tok):
            assert img_tok % 3 == 0, 'Invalid text token sizes'
            sit = img_tok // 3
            N = txt_tok + img_tok
            i = jnp.arange(N)[:, None]
            j = jnp.arange(N)[None, :]
            img_img = (i < img_tok) & (j < img_tok) & (i // sit == j // sit)
            txt_img = (i >= img_tok) & (j < img_tok)
            txt_txt = (i >= img_tok) & (j >= img_tok) & (i >= j)
            return img_img | txt_img | txt_txt
        B, N, C = q.shape
        H = NUM_HEADS
        d = C // H
        scale = d ** (-0.5)
        qh = (q @ Wq + bq).reshape(B, N, H, d).transpose(0, 2, 1, 3)
        kh = (kv @ Wk + bk).reshape(B, N, H, d).transpose(0, 2, 1, 3)
        vh = (kv @ Wv + bv).reshape(B, N, H, d).transpose(0, 2, 1, 3)
        scores = jnp.einsum('bhqd,bhkd->bhqk', qh, kh) * scale
        mask = trinity_mask(txt_tok_len, img_tok_len)
        scores = jnp.where(mask[None, None], scores, -jnp.inf)
        attn = jax.nn.softmax(scores, axis=-1)
        out = jnp.einsum('bhqk,bhkd->bhqd', attn, vh)
        out = out.transpose(0, 2, 1, 3).reshape(B, N, C)
        return out @ Wo + bo

    def _L0_ffn_ref(x, weight, bias):
        import jax, jax.numpy as jnp
        import numpy as np
        BLOCK_SIZE = 32
        FP6_E2M3_MAX = 7.5

        def _build_fp6_e2m3_grid():
            vals = set()
            for bits in range(64):
                s = bits >> 5 & 1
                e = bits >> 3 & 3
                m = bits & 7
                v = m / 8.0 if e == 0 else (1.0 + m / 8.0) * 2.0 ** (e - 1)
                vals.add(-v if s else v)
            return np.array(sorted(vals), dtype=np.float32)
        _GRID = jnp.asarray(_build_fp6_e2m3_grid())

        def _nearest_on_grid(x, grid):
            idx = jnp.clip(jnp.searchsorted(grid, x), 0, grid.shape[0] - 1)
            idx_lo = jnp.maximum(idx - 1, 0)
            v_hi = grid[idx]
            v_lo = grid[idx_lo]
            return jnp.where(jnp.abs(x - v_lo) <= jnp.abs(x - v_hi), v_lo, v_hi)

        def _mx_quantize(t, eps=1e-30):
            rows, K = t.shape
            blocks = t.reshape(rows, K // BLOCK_SIZE, BLOCK_SIZE)
            scales = jnp.maximum(jnp.max(jnp.abs(blocks), axis=-1) / FP6_E2M3_MAX, eps)
            q = _nearest_on_grid(blocks / scales[..., None], _GRID)
            return (q, scales)
        batch_shape = x.shape[:-1]
        in_features = x.shape[-1]
        x2 = x.astype(jnp.float32).reshape(-1, in_features)
        w2 = weight.astype(jnp.float32)
        xq, xs = _mx_quantize(x2)
        wq, ws = _mx_quantize(w2)
        xd = (xq * xs[..., None]).reshape(x2.shape)
        wd = (wq * ws[..., None]).reshape(w2.shape)
        out = xd @ wd.T + bias
        return out.reshape(*batch_shape, -1)

    def _L1_xattn_ref(tgt, mem, attn_bias, memory_key_padding_mask, Wq_w, Wq_b, Wkv_w, Wkv_b, out_w, out_b):
        import jax, jax.numpy as jnp
        import numpy as np
        EMBED_DIM = 128
        NUM_HEADS = 16
        HEAD_DIM = EMBED_DIM // NUM_HEADS
        B, SQ, SK = (2, 256, 256)
        b, sq, _ = tgt.shape
        sk = mem.shape[1]
        q = (tgt @ Wq_w.T + Wq_b).reshape(b, sq, NUM_HEADS, HEAD_DIM)
        kv = (mem @ Wkv_w.T + Wkv_b).reshape(b, sk, 2, NUM_HEADS, HEAD_DIM)
        k, v = (kv[:, :, 0], kv[:, :, 1])
        scale = 1.0 / np.sqrt(HEAD_DIM)
        scores = jnp.einsum('bthd,bshd->bhts', q, k * scale)
        scores = scores + attn_bias[:, None, None, :]
        pad = jnp.where(memory_key_padding_mask, 0.0, -jnp.inf).astype(scores.dtype)
        scores = scores + pad[:, None, None, :]
        attn = jax.nn.softmax(scores, axis=-1)
        ctx = jnp.einsum('bhts,bshd->bthd', attn, v)
        out = ctx.reshape(b, sq, EMBED_DIM) @ out_w.T + out_b
        return out

    def _L1_ffn_ref(tgt, Wr, br, W1, b1, W2, b2, gamma, beta):
        import jax, jax.numpy as jnp
        import numpy as np
        B, S, D, F, E = (2, 256, 128, 512, 8)
        LN_EPS = 1e-05

        def _layer_norm(x, gamma, beta):
            mu = jnp.mean(x, axis=-1, keepdims=True)
            var = jnp.mean(jnp.square(x - mu), axis=-1, keepdims=True)
            return (x - mu) * jax.lax.rsqrt(var + LN_EPS) * gamma + beta
        logits = jnp.einsum('bsd,ed->bse', tgt, Wr) + br
        top_v, top_i = jax.lax.top_k(logits, 2)
        top_w = jax.nn.softmax(top_v, axis=-1)
        n_exp = logits.shape[-1]
        router_w = jnp.sum(jax.nn.one_hot(top_i, n_exp, dtype=top_w.dtype) * top_w[..., None], axis=-2)
        h = jnp.einsum('bsd,efd->bsef', tgt, W1) + b1
        h = jax.nn.relu(h)
        o = jnp.einsum('bsef,edf->bsed', h, W2) + b2
        tgt2 = jnp.einsum('bsed,bse->bsd', o, router_w)
        return _layer_norm(tgt + tgt2, gamma, beta)
    x = x + jnp.tanh(g_xattn[0]) * _L0_xattn_ref(_layernorm(x, axis=-1), ctx_1024, L0_xattn_Wq, L0_xattn_bq, L0_xattn_Wk, L0_xattn_bk, L0_xattn_Wv, L0_xattn_bv, L0_xattn_Wo, L0_xattn_bo, 64, 192)
    x = x + jnp.tanh(g_ffn[0]) * _L0_ffn_ref(_layernorm(x, axis=-1), L0_ffn_weight, L0_ffn_bias)
    x = x + jnp.tanh(g_xattn[1]) * _L1_xattn_ref(_layernorm(x, axis=-1), ctx_1024, fside_BxS2_0, mask_BxS2_bk0, L1_xattn_Wq_w, L1_xattn_Wq_b, L1_xattn_Wkv_w, L1_xattn_Wkv_b, L1_xattn_out_w, L1_xattn_out_b)
    x = x + jnp.tanh(g_ffn[1]) * _L1_ffn_ref(_layernorm(x, axis=-1), L1_ffn_Wr, L1_ffn_br, L1_ffn_W1, L1_ffn_b1, L1_ffn_W2, L1_ffn_b2, L1_ffn_gamma, L1_ffn_beta)
    return x

_drawn_inputs = setup_inputs


def setup_inputs(seed=0):
    import zlib

    import numpy as np

    out = dict(_drawn_inputs(seed))
    spreads = {'g_ffn': (-1.0, 0.2),
     'L0_xattn_bq': (0.0, 0.1),
     'L0_xattn_bk': (0.0, 0.1),
     'L0_xattn_bv': (0.0, 0.1),
     'L0_xattn_bo': (0.0, 0.1),
     'L1_xattn_Wq_b': (0.0, 0.1),
     'L1_xattn_Wkv_b': (0.0, 0.1),
     'L1_xattn_out_b': (0.0, 0.1),
     'L1_ffn_br': (0.0, 0.1),
     'L1_ffn_b1': (0.0, 0.1),
     'L1_ffn_b2': (0.0, 0.1),
     'L1_ffn_gamma': (1.0, 0.2),
     'L1_ffn_beta': (0.0, 0.1)}
    factors = {}
    for name, (base, spread) in spreads.items():
        noise = np.random.default_rng([zlib.crc32(name.encode()), seed]).standard_normal(out[name].shape)
        drawn = base * np.exp(spread * noise) if base else spread * noise
        out[name] = jnp.asarray(drawn.astype(out[name].dtype))
    for name, factor in factors.items():
        out[name] = (out[name] * factor).astype(out[name].dtype)
    return out
```

```python
import numpy as np
import concourse.bass as bass
from concourse import mybir
from contextlib import ExitStack

F32 = mybir.dt.float32
F32R = mybir.dt.float32r
I32 = mybir.dt.int32
U32 = mybir.dt.uint32
U8 = mybir.dt.uint8
ALU = mybir.AluOpType
ACT = mybir.ActivationFunctionType
AX = mybir.AxisListType.X

B, S, D, H, E, F = 8, 256, 128, 16, 8, 512
HD = D // H
NB = D // 32
FB = F // 128
SCALE = HD ** -0.5
FAR = 1e30
EPS = 1e-5
ROW_MAX, ROW_BIAS = 24, 25

CONST_COLS = [("ident", 128), ("sel", 4 * 4 * 128), ("auxsel", 128), ("causal", 64), ("wsel", E * 128),
              ("qaux", 1), ("kaux", 1), ("iota", E), ("b1", E * FB), ("b2", E), ("bq", 2), ("bk", 2),
              ("gates", 4), ("bv", 2 * 128), ("ffn_b", 128), ("gamma", 128), ("beta", 128), ("br", E)]
CONST_AT, _n = {}, 0
for _name, _w in CONST_COLS:
    CONST_AT[_name] = (_n, _n + _w)
    _n += _w
NCONST = _n
N_ROUNDED = CONST_AT["wsel"][1]


def program(nc, x, ctx_in, side_col, mask_col, side_row, mask_row, const, w_attn, w_ffn, w_router, w1, w2, out):
    stack = ExitStack()
    with stack:
        def sb(name, shape, dt=F32):
            return stack.enter_context(nc.sbuf_tensor(name, shape, dt))

        def sem(name):
            return stack.enter_context(nc.semaphore(name))

        cst = sb("cst", [128, NCONST])
        rnd = sb("rnd", [128, N_ROUNDED], F32R)

        def c(name):
            a, b = CONST_AT[name]
            return cst[:, a:b]

        def cr(name):
            a, b = CONST_AT[name]
            return rnd[:, a:b]

        ident = c("ident")
        sel = cr("sel").rearrange("p (k t m) -> p k t m", k=4, t=4)
        wsel = cr("wsel").rearrange("p (e m) -> p e m", e=E)
        wat = sb("wat", [128, 2, 5, 128])
        wfr = sb("wfr", [128, 128])
        wdq = sb("wdq", [128, 128])
        wdT = sb("wdT", [128, 128])
        wrT = sb("wrT", [128, E])
        w1s = sb("w1s", [128, E * FB, 128])
        w2s = sb("w2s", [128, E * FB, 128])
        gate = sb("gate", [128, 4])
        gfb = sb("gfb", [128, 128])
        ggam = sb("ggam", [128, 128])
        gbet = sb("gbet", [128, 128])
        halfs = sb("halfs", [128, 2])
        sidec = sb("sidec", [128, B, 2])
        maskc = sb("maskc", [128, B, 2], U8)
        keepc = sb("keepc", [128, B, 2])
        penc = sb("penc", [128, B, 2])
        kbc = sb("kbc", [128, B, 2], F32R)
        ebc = sb("ebc", [128, B, 2])
        ebias = sb("ebias", [128, 2])
        sider = sb("sider", [1, B * S])
        maskr = sb("maskr", [1, B * S], U8)
        keepr = sb("keepr", [1, B * S])
        penr = sb("penr", [1, B * S])
        kbr = sb("kbr", [1, B * S], F32R)
        kbrow = sb("kbrow", [1, S], F32R)

        xin = sb("xin", [128, 2, D])
        cin = sb("cin", [128, 2, D])
        x1 = sb("x1", [128, 2, D])
        x1b = sb("x1b", [128, 2, D])
        x2 = sb("x2", [128, 2, D])
        x3 = sb("x3", [128, 2, D])
        x3n = sb("x3n", [128, 2, D])
        stats = sb("stats", [128, 2, 6])
        mv = sb("mv", [128, 2, 2])
        veps = sb("veps", [128, 2])
        rstd = sb("rstd", [128, 2])
        xn = sb("xn", [128, 2, D])
        xnT = sb("xnT", [128, S])
        ctxT = sb("ctxT", [128, S])
        qh = sb("qh", [128, S], F32R)
        ql = sb("ql", [128, S], F32R)
        kh = sb("kh", [128, S], F32R)
        kl = sb("kl", [128, S], F32R)
        qs = sb("qs", [128, 4, S], F32R)
        ks = sb("ks", [128, 4, S], F32R)
        vst = sb("vst", [128, 2, H, 32])
        mx = sb("mx", [128, 2, 4, 4])
        mneg = sb("mneg", [H, S], F32R)
        P = sb("P", [128, 2, 4, 4, S])
        sh = sb("sh", [128, 2 * S])
        rsh = sb("rsh", [128, 2 * S])
        on = sb("on", [128, 2, S])
        bmax = sb("bmax", [128, 2 * NB])
        scl = sb("scl", [128, 2 * NB])
        rscl = sb("rscl", [128, 2 * NB])
        yq = sb("yq", [128, 2 * NB, 32])
        eb = sb("eb", [128, 2 * NB, 32], I32)
        ib = sb("ib", [128, 2 * NB, 32], I32)
        pb = sb("pb", [128, 2 * NB, 32], I32)
        zq = sb("zq", [128, 2 * NB, 32])
        rq = sb("rq", [128, 2 * NB, 32])
        dq = sb("dq", [128, 2 * NB, 32])
        nq = sb("nq", [128, 2 * NB, 32])
        ps_ = sb("ps_", [128, 2 * NB, 32])
        xd = sb("xd", [128, 2 * NB, 32])
        xdT = sb("xdT", [128, S])
        x3T = sb("x3T", [128, S])
        xb3 = sb("xb3", [128, 2, D])
        lg = sb("lg", [128, 2, E])
        top = sb("top", [128, 2, 8])
        topi = sb("topi", [128, 2, 8], U32)
        topf = sb("topf", [128, 2, 8])
        gap = sb("gap", [128, 2, 1])
        egap = sb("egap", [128, 2, 1])
        den = sb("den", [128, 2, 1])
        tw = sb("tw", [128, 2, 2])
        r1 = sb("r1", [128, 2, E])
        r2 = sb("r2", [128, 2, E])
        rw = sb("rw", [128, 2, E])
        wc = sb("wc", [128, 2, 2 * E], F32R)
        wT = sb("wT", [2 * E, S], F32R)
        wbc = sb("wbc", [128, E, S])
        hbuf = sb("hbuf", [128, 2, FB, S])
        te = sb("te", [128, 2, S])
        acc = sb("acc", [128, S])
        zst = sb("zst", [128, 2, 6])
        zmv = sb("zmv", [128, 2, 2])
        zve = sb("zve", [128, 2])
        zrs = sb("zrs", [128, 2])
        zn = sb("zn", [128, 2, D])
        zg = sb("zg", [128, 2, D])
        outt = sb("outt", [128, 2, D])

        SC = stack.enter_context(nc.psum_tensor("SC", [128, 4, 512], F32))
        PV = stack.enter_context(nc.psum_tensor("PV", [128, 512], F32))
        HP = stack.enter_context(nc.psum_tensor("HP", [128, 2, 512], F32))
        OP = stack.enter_context(nc.psum_tensor("OP", [128, 512], F32))

        names = """apart const_in attn_w_in ffn_w_in router_w_in w1_in w2_in side_in x_in ctx_in_ rounded ones_set v_zero
            gates_done prep_step pool_prep bias_prep wd_quant wdT_ps wdT_sb batch_bias
            ln_stats ln_veps ln_rstd xn_sb ctxT_ps ctxT_sb k_ps v_ps xnT_ps xnT_sb q_ps k_hi q_hi k_lo q_lo v_sb
            kstack_ps qstack_ps kstack_sb qstack_sb s_ps s_max mxT_ps mneg_sb max_row st_ps exp_sb p_masked
            pv_ps on_sb y_ps x_res x1b_sb xd_sb xdT_ps xdT_sb ffn_ps attn_step quant_d
            x3T_ps x3T_sb xb3_sb logits_ps gap_sb egap_sb weights_sb wT_ps wT_sb wbc_ps wbc_sb h_ps relu_sb o_ps
            te_sb acc_sb zT_ps z_stats z_veps z_rstd zn_sb out_sb stored moe_step""".split()
        s = {n: sem(n) for n in names}

        ATTN_STEPS, MOE_STEPS = 24, 14

        def first_of(b):
            return isinstance(b, int) and b == 0

        def counted(eng, semaphore, base):
            n = [0]

            def done(ins):
                n[0] += 1
                return ins.then_inc(semaphore, 1)

            def settle(apart=False):
                (wait_apart(eng, semaphore, base + n[0]) if apart else eng.wait_ge(semaphore, base + n[0]))
            return done, settle, n

        def wait_apart(eng, semaphore, value):
            eng.wait_ge(semaphore, value)
            if not isinstance(value, int):
                eng.sem_inc(s["apart"])

        def quantize(dve, done, settle, src, nb, dst, last=None):
            def bc(t):
                return t[:, 0:nb].unsqueeze(2).to_broadcast([128, nb, 32])
            v = slice(0, nb)
            done(dve.tensor_reduce(bmax[:, v], src, AX, ALU.max, apply_absolute_value=True))
            settle()
            done(dve.tensor_scalar(scl[:, v], bmax[:, v], 1.0 / 7.5, 1e-30, ALU.mult, ALU.max))
            settle()
            done(dve.reciprocal(rscl[:, v], scl[:, v]))
            settle()
            done(dve.tensor_tensor(yq[:, v], src, bc(rscl), ALU.mult))
            settle()
            done(dve.tensor_scalar(eb[:, v], yq[:, v].bitcast(I32), 0x7F800000, None, ALU.bitwise_and))
            settle()
            done(dve.tensor_scalar(pb[:, v].bitcast(F32), eb[:, v].bitcast(F32), 1.0, 4.0, ALU.max, ALU.min))
            settle()
            done(dve.tensor_scalar(ib[:, v], pb[:, v], -1.0, float(257 << 23), ALU.mult, ALU.add))
            done(dve.tensor_tensor(ps_[:, v], pb[:, v].bitcast(F32), bc(scl), ALU.mult))
            settle()
            done(dve.tensor_tensor(zq[:, v], yq[:, v], ib[:, v].bitcast(F32), ALU.mult))
            settle()
            done(dve.tensor_scalar(rq[:, v], zq[:, v], 12582912.0, -12582912.0, ALU.add, ALU.add))
            settle()
            done(dve.tensor_tensor(dq[:, v], rq[:, v], zq[:, v], ALU.subtract))
            settle()
            done(dve.scalar_tensor_tensor(nq[:, v], dq[:, v], 0.5, rq[:, v], ALU.is_ge, ALU.subtract))
            settle()
            ins = dve.scalar_tensor_tensor(dst, nq[:, v], -0.125, ps_[:, v], ALU.mult, ALU.mult)
            (ins.then_inc(last, 1) if last is not None else done(ins))

        def q_range(l, kt):
            return (0, S) if l == 1 else ((0, 192), (128, 256))[kt]

        def unit(n):
            return n // 4, (n // 2) % 2, n % 2

        block = stack.enter_context(nc.Block())

        @block.sync
        def _(sp):
            def load(b):
                sp.dma_start(xin[:], x[:, bass.ds(b, 1)].rearrange("p o q d -> p (o q) d")).then_inc(s["x_in"], 16)
                sp.dma_start(cin[:], ctx_in[:, bass.ds(b, 1)].rearrange("p o q d -> p (o q) d")).then_inc(s["ctx_in_"], 16)

            def max_rows(b, l):
                sp.wait_ge(s["mneg_sb"], b * 2 + l + 1)
                for i in range(4):
                    r = 32 * i + ROW_MAX
                    sp.dma_start(qs[r:r + 1, :, :].bitcast(F32), mneg[4 * i:4 * i + 4, :].bitcast(F32)).then_inc(s["max_row"], 16)

            def attn(b, more):
                max_rows(b, 0)
                if more:
                    sp.wait_ge(s["ctxT_ps"], b + 1)
                    wait_apart(sp, s["x_res"], 3 * b + 1)
                    load(b + 1)
                max_rows(b, 1)

            def store(m):
                wait_apart(sp, s["out_sb"], m + 2)
                sp.dma_start(out[:, bass.ds(m, 1)].rearrange("p o q d -> p (o q) d"), outt[:]).then_inc(s["stored"], 16)

            sp.sem_inc(s["stored"], 16)
            sp.dma_start(cst[:], const).then_inc(s["const_in"], 16)
            load(0)
            sp.dma_start(wat[:], w_attn).then_inc(s["attn_w_in"], 16)
            sp.dma_start(wfr[:], w_ffn).then_inc(s["ffn_w_in"], 16)
            for dst, src in ((sidec, side_col), (maskc, mask_col), (sider, side_row), (maskr, mask_row)):
                sp.dma_start(dst[:], src).then_inc(s["side_in"], 16)
            sp.dma_start(wrT[:], w_router).then_inc(s["router_w_in"], 16)
            sp.dma_start(w1s[:], w1).then_inc(s["w1_in"], 16)
            sp.dma_start(w2s[:], w2).then_inc(s["w2_in"], 16)
            attn(0, True)
            with sp.Fori(0, B - 2) as m:
                attn(m + 1, True)
                store(m)
            attn(B - 1, False)
            store(B - 2)
            store(B - 1)
            sp.wait_ge(s["stored"], 16 * B + 16)

        @block.tensor
        def _(pe):
            def transpose2(dst, src):
                for t in range(2):
                    last = pe.transpose(dst[:, t * 128:(t + 1) * 128], src[:, t * 128:(t + 1) * 128], ident)
                return last

            def front(b, l):
                if l == 0:
                    pe.wait_ge(s["ctx_in_"], 16 * b + 16)
                    transpose2(SC[:, 1], cin[:].rearrange("p q d -> p (q d)")).then_inc(s["ctxT_ps"], 1)
                    pe.wait_ge(s["ctxT_sb"], b + 1)
                pe.matmul(SC[:, 3, 0:S], wat[:, l, 1], ctxT[:], start=True, stop=True).then_inc(s["k_ps"], 1)
                for t in range(2):
                    last = pe.matmul(SC[:, 1, t * 128:(t + 1) * 128], ctxT[:, t * 128:(t + 1) * 128], wat[:, l, 2],
                                     start=True, stop=True)
                last.then_inc(s["v_ps"], 1)
                pe.wait_ge(s["xn_sb"], 4 * b + 1 + 2 * l)
                transpose2(SC[:, 0], xn[:].rearrange("p q d -> p (q d)")).then_inc(s["xnT_ps"], 1)
                pe.wait_ge(s["xnT_sb"], 2 * b + l + 1)
                pe.matmul(SC[:, 2, 0:S], wat[:, l, 0], xnT[:], start=True, stop=True).then_inc(s["q_ps"], 1)

            def stacks(b, l):
                pe.wait_ge(s["k_lo"], 2 * b + l + 1)
                if l == 1:
                    pe.wait_ge(s["batch_bias"], 2 * b + 2)
                for half, bank in ((0, 3), (1, 0)):
                    for tt in range(2):
                        o = SC[:, bank, tt * S:(tt + 1) * S]
                        t = 2 * half + tt
                        pe.matmul(o, sel[:, 2, t], kh[:], start=True, stop=False)
                        last = pe.matmul(o, sel[:, 3, t], kl[:], start=False, stop=l == 0)
                        if l == 1:
                            last = pe.matmul(o, cr("auxsel")[0:1, :], kbrow[:], start=False, stop=True)
                    last.then_inc(s["kstack_ps"], 1)
                pe.wait_ge(s["q_lo"], 2 * b + l + 1)
                pe.wait_ge(s["v_sb"], 4 * b + 2 * l + 2)
                for half, bank in ((0, 2), (1, 1)):
                    for tt in range(2):
                        o = SC[:, bank, tt * S:(tt + 1) * S]
                        t = 2 * half + tt
                        pe.matmul(o, sel[:, 0, t], qh[:], start=True, stop=False)
                        last = pe.matmul(o, sel[:, 1, t], ql[:], start=False, stop=True)
                    last.then_inc(s["qstack_ps"], 1)

            def scores(b, l):
                pe.wait_ge(s["kstack_sb"], 4 * b + 2 * l + 2)
                pe.wait_ge(s["qstack_sb"], 4 * b + 2 * l + 2)
                for n in range(8):
                    qt, tp, u = unit(n)
                    if n >= 2:
                        pe.wait_ge(s["s_max"], 16 * b + 8 * l + n - 1)
                    nk = 128 if l == 0 and qt == 0 else S
                    for tt in range(2):
                        for i in (2 * u, 2 * u + 1):
                            r = slice(32 * i, 32 * i + 32)
                            masked = l == 0 and qt == 1
                            last = pe.matmul(SC[:, i, tt * S:tt * S + nk], qs[r, 2 * tp + tt, qt * 128:qt * 128 + 128],
                                             ks[r, 2 * tp + tt, 0:nk], start=True, stop=not masked)
                            if masked:
                                last = pe.matmul(SC[:, i, tt * S + 128:tt * S + 192], cr("ident"), cr("causal"),
                                                 start=False, stop=True)
                    last.then_inc(s["s_ps"], 1)

            def max_out(b, l):
                pe.wait_ge(s["s_max"], 16 * b + 8 * l + 8)
                for qt in range(2):
                    last = pe.transpose(PV[0:H, qt * 128:qt * 128 + 128], mx[:, qt].rearrange("p i t -> p (i t)"), ident)
                last.then_inc(s["mxT_ps"], 1)

            def weigh(b, l, n):
                tp, kt, u = unit(n)
                if l == 0:
                    pe.wait_ge(s["p_masked"], 16 * b + 2 * n + 2)
                else:
                    pe.wait_ge(s["exp_sb"], 16 * b + 8 + n + 1)
                parts = [q_range(l, kt)] if l == 1 or kt == 0 else [(128, 192), (192, 256)]
                for tt in range(2):
                    for ii in range(2):
                        i, t, j = 2 * u + ii, 2 * tp + tt, 2 * ii + tt
                        for a, z in parts:
                            last = pe.matmul(PV[32 * j:32 * j + 32, tp * S + a:tp * S + z], vst[:, kt, 4 * i + t],
                                             P[:, kt, 2 * tp + u, 2 * ii + tt, a:z], start=(kt == 0 and u == 0),
                                             stop=(kt == 1 and u == 1), skip_group_check=True)
                if kt == 1 and u == 1:
                    last.then_inc(s["pv_ps"], 1)

            def attend(b, l):
                pe.wait_ge(s["max_row"], 128 * b + 64 * l + 64)
                for n in range(8):
                    tp, kt, u = unit(n)
                    if n >= 2:
                        pe.wait_ge(s["exp_sb"], 16 * b + 8 * l + n - 1)
                    a, z = q_range(l, kt)
                    for tt in range(2):
                        for i in (2 * u, 2 * u + 1):
                            r = slice(32 * i, 32 * i + 32)
                            last = pe.matmul(SC[:, i, tt * S:tt * S + z - a], ks[r, 2 * tp + tt, kt * 128:kt * 128 + 128],
                                             qs[r, 2 * tp + tt, a:z], start=True, stop=True)
                    last.then_inc(s["st_ps"], 1)
                    if n >= 1:
                        weigh(b, l, n - 1)
                weigh(b, l, 7)

            def project(b, l):
                pe.wait_ge(s["on_sb"], 2 * b + l + 1)
                for qt in range(2):
                    for ab in range(2):
                        last = pe.matmul(SC[:, 0, qt * 128:qt * 128 + 128], on[:, ab, qt * 128:qt * 128 + 128],
                                         wat[:, l, 3 + ab], start=(ab == 0), stop=(ab == 1))
                last.then_inc(s["y_ps"], 1)

            def ffn_turn(b):
                pe.wait_ge(s["xd_sb"], b + 1)
                transpose2(SC[:, 1], xd[:].rearrange("p n k -> p (n k)")).then_inc(s["xdT_ps"], 1)

            def ffn_out(b):
                pe.wait_ge(s["xdT_sb"], b + 1)
                for qt in range(2):
                    last = pe.matmul(SC[:, 2, qt * 128:qt * 128 + 128], xdT[:, qt * 128:qt * 128 + 128], wdT[:],
                                     start=True, stop=True)
                last.then_inc(s["ffn_ps"], 1)

            def moe_in(m):
                pe.wait_ge(s["xn_sb"], 4 * m + 4)
                transpose2(HP[:, 0], x3n[:].rearrange("p q d -> p (q d)")).then_inc(s["x3T_ps"], 1)
                pe.wait_ge(s["x3T_sb"], m + 1)
                for qt in range(2):
                    last = pe.matmul(OP[:, qt * E:qt * E + E], x3T[:, qt * 128:qt * 128 + 128], wrT[:],
                                     start=True, stop=True)
                last.then_inc(s["logits_ps"], 1)

            def moe_weights(m):
                pe.wait_ge(s["weights_sb"], m + 1)
                for qt in range(2):
                    last = pe.transpose(OP[0:2 * E, S + qt * 128:S + qt * 128 + 128], wc[:, qt].bitcast(F32), ident)
                last.then_inc(s["wT_ps"], 1)
                pe.wait_ge(s["wT_sb"], m + 1)
                for g in range(4):
                    if g >= 2:
                        pe.wait_ge(s["wbc_sb"], 4 * m + g - 1)
                    for e in (2 * g, 2 * g + 1):
                        last = pe.matmul(HP[:, g % 2, (e % 2) * S:(e % 2) * S + S], wsel[0:2 * E, e], wT[:],
                                         start=True, stop=True)
                    last.then_inc(s["wbc_ps"], 1)

            def slot(m, n):
                if n < E:
                    for p in range(2):
                        if n == 0:
                            pe.wait_ge(s["wbc_sb"], 4 * m + 3 + p)
                        else:
                            pe.wait_ge(s["relu_sb"], 4 * E * m + 4 * (n - 1) + 2 * p + 2)
                        for k in range(2):
                            last = pe.matmul(HP[:, p, k * S:(k + 1) * S], w1s[:, FB * n + 2 * p + k], x3T[:],
                                             start=True, stop=True)
                        last.then_inc(s["h_ps"], 1)
                if n >= 1:
                    e = n - 1
                    if e >= 1:
                        pe.wait_ge(s["te_sb"], E * m + e)
                    pe.wait_ge(s["relu_sb"], 4 * E * m + 4 * e + 4)
                    for k in range(FB):
                        last = pe.matmul(OP[:, 0:S], w2s[:, FB * e + k], hbuf[:, e % 2, k], start=(k == 0), stop=(k == FB - 1))
                    last.then_inc(s["o_ps"], 1)

            def moe_out(m):
                pe.wait_ge(s["acc_sb"], E * m + E)
                transpose2(OP, acc[:]).then_inc(s["zT_ps"], 1)

            def both(b, m):
                moe_in(m)
                front(b, 0)
                moe_weights(m)
                stacks(b, 0)
                slot(m, 0)
                scores(b, 0)
                max_out(b, 0)
                slot(m, 1)
                attend(b, 0)
                slot(m, 2)
                project(b, 0)
                slot(m, 3)
                slot(m, 4)
                ffn_turn(b)
                slot(m, 5)
                ffn_out(b)
                slot(m, 6)
                front(b, 1)
                slot(m, 7)
                stacks(b, 1)
                scores(b, 1)
                max_out(b, 1)
                slot(m, 8)
                attend(b, 1)
                moe_out(m)
                project(b, 1)

            pe.wait_ge(s["const_in"], 16)
            pe.wait_ge(s["attn_w_in"], 16)
            pe.wait_ge(s["rounded"], 1)
            front(0, 0)
            stacks(0, 0)
            scores(0, 0)
            max_out(0, 0)
            attend(0, 0)
            project(0, 0)
            pe.wait_ge(s["wd_quant"], 1)
            pe.transpose(SC[:, 3, 0:128], wdq[:], ident).then_inc(s["wdT_ps"], 1)
            ffn_turn(0)
            pe.wait_ge(s["wdT_sb"], 1)
            ffn_out(0)
            front(0, 1)
            stacks(0, 1)
            scores(0, 1)
            max_out(0, 1)
            attend(0, 1)
            project(0, 1)
            pe.wait_ge(s["router_w_in"], 16)
            pe.wait_ge(s["w1_in"], 16)
            pe.wait_ge(s["w2_in"], 16)
            with pe.Fori(0, B - 1) as m:
                both(m + 1, m)
            moe_in(B - 1)
            moe_weights(B - 1)
            for n in range(E + 1):
                slot(B - 1, n)
            moe_out(B - 1)

        @block.scalar
        def _(act):
            def front(b, l):
                if l == 0:
                    act.wait_ge(s["ctxT_ps"], b + 1)
                    act.activation(ctxT[:], SC[:, 1, 0:S], ACT.Copy).then_inc(s["ctxT_sb"], 1)
                act.wait_ge(s["k_ps"], 2 * b + l + 1)
                act.activation(kh[:], SC[:, 3, 0:S], ACT.Identity, bias=c("bk")[:, l:l + 1]).then_inc(s["k_hi"], 1)
                act.wait_ge(s["xnT_ps"], 2 * b + l + 1)
                act.activation(xnT[:], SC[:, 0, 0:S], ACT.Copy).then_inc(s["xnT_sb"], 1)
                act.wait_ge(s["q_ps"], 2 * b + l + 1)
                act.activation(qh[:], SC[:, 2, 0:S], ACT.Identity, bias=c("bq")[:, l:l + 1]).then_inc(s["q_hi"], 1)

            def stacks(b, l):
                for half, bank in ((0, 3), (1, 0)):
                    act.wait_ge(s["kstack_ps"], 4 * b + 2 * l + half + 1)
                    act.activation(ks[:, 2 * half:2 * half + 2].rearrange("p t k -> p (t k)"), SC[:, bank],
                                   ACT.Identity, bias=c("kaux")).then_inc(s["kstack_sb"], 1)

            def max_out(b, l):
                act.wait_ge(s["mxT_ps"], 2 * b + l + 1)
                act.activation(mneg[:], PV[0:H, 0:S], ACT.Copy, scale=-1.0).then_inc(s["mneg_sb"], 1)

            def attend(b, l):
                for n in range(8):
                    tp, kt, u = unit(n)
                    a, z = q_range(l, kt)
                    act.wait_ge(s["st_ps"], 16 * b + 8 * l + n + 1)
                    scores = SC[:, 2 * u:2 * u + 2].rearrange("p i (t q) -> p i t q", t=2)[:, :, :, 0:z - a]
                    more = {"bias": ebias[:, kt:kt + 1]} if l == 1 else {}
                    act.activation(P[:, kt, 2 * tp + u, :, a:z].rearrange("p (i t) q -> p i t q", i=2), scores, ACT.Exp, scale=SCALE,
                                   **more).then_inc(s["exp_sb"], 1)

            def ffn(b):
                act.wait_ge(s["xdT_ps"], b + 1)
                act.activation(xdT[:], SC[:, 1, 0:S], ACT.Copy).then_inc(s["xdT_sb"], 1)

            def moe_in(m):
                act.wait_ge(s["x3T_ps"], m + 1)
                act.activation(x3T[:], HP[:, 0, 0:S], ACT.Copy).then_inc(s["x3T_sb"], 1)

            def moe_gap(m):
                act.wait_ge(s["gap_sb"], m + 1)
                act.activation(egap[:], gap[:], ACT.Exp).then_inc(s["egap_sb"], 1)

            def moe_weights(m):
                act.wait_ge(s["wT_ps"], m + 1)
                act.activation(wT[:], OP[0:2 * E, S:2 * S], ACT.Copy).then_inc(s["wT_sb"], 1)
                for g in range(4):
                    act.wait_ge(s["wbc_ps"], 4 * m + g + 1)
                    act.activation(wbc[:, 2 * g:2 * g + 2].rearrange("p e q -> p (e q)"), HP[:, g % 2],
                                   ACT.Copy).then_inc(s["wbc_sb"], 1)

            def slot(m, n):
                if n < E:
                    if n >= 2:
                        act.wait_ge(s["o_ps"], E * m + n - 1)
                    for k in range(FB):
                        if k % 2 == 0:
                            act.wait_ge(s["h_ps"], 2 * E * m + 2 * n + k // 2 + 1)
                        act.activation(hbuf[:, n % 2, k], HP[:, k // 2, (k % 2) * S:(k % 2) * S + S], ACT.Relu,
                                       bias=c("b1")[:, FB * n + k:FB * n + k + 1]).then_inc(s["relu_sb"], 1)

            def both(b, m):
                moe_in(m)
                front(b, 0)
                moe_gap(m)
                moe_weights(m)
                stacks(b, 0)
                slot(m, 0)
                max_out(b, 0)
                slot(m, 1)
                attend(b, 0)
                slot(m, 2)
                slot(m, 3)
                slot(m, 4)
                ffn(b)
                slot(m, 5)
                slot(m, 6)
                front(b, 1)
                slot(m, 7)
                stacks(b, 1)
                max_out(b, 1)
                attend(b, 1)

            act.wait_ge(s["const_in"], 16)
            act.activation(gate[:], c("gates"), ACT.Tanh).then_inc(s["gates_done"], 1)
            front(0, 0)
            stacks(0, 0)
            max_out(0, 0)
            attend(0, 0)
            act.wait_ge(s["wdT_ps"], 1)
            act.activation(wdT[:], SC[:, 3, 0:128], ACT.Copy).then_inc(s["wdT_sb"], 1)
            ffn(0)
            front(0, 1)
            stacks(0, 1)
            max_out(0, 1)
            attend(0, 1)
            with act.Fori(0, B - 1) as m:
                both(m + 1, m)
            moe_in(B - 1)
            moe_gap(B - 1)
            moe_weights(B - 1)
            for n in range(E):
                slot(B - 1, n)

        @block.vector
        def _(dve):
            def layer_norm(src, k, done, settle, dst=xn):
                for qt in range(2):
                    done(dve.bn_stats(stats[:, qt], src[:, qt]))
                settle(apart=True)
                for qt in range(2):
                    last = dve.bn_aggr(mv[:, qt], stats[:, qt])
                last.then_inc(s["ln_stats"], 1)
                dve.wait_ge(s["ln_rstd"], k)
                for qt in range(2):
                    last = dve.tensor_scalar(dst[:, qt], src[:, qt], mv[:, qt, 0:1], rstd[:, qt:qt + 1],
                                             ALU.subtract, ALU.mult)
                last.then_inc(s["xn_sb"], 1)

            def batch_bias(b):
                dve.tensor_copy(ebias[:], ebc[:, bass.ds(b, 1)].rearrange("p o k -> p (o k)")).then_inc(s["batch_bias"], 1)
                dve.tensor_copy(kbrow[:], kbr[:, bass.ds(b * S, S)].bitcast(F32)).then_inc(s["batch_bias"], 1)

            def front(b, l):
                dve.wait_ge(s["k_hi"], 2 * b + l + 1)
                dve.scalar_tensor_tensor(kl[:], SC[:, 3, 0:S], c("bk")[:, l:l + 1], kh[:].bitcast(F32),
                                         ALU.add, ALU.subtract).then_inc(s["k_lo"], 1)
                dve.wait_ge(s["v_ps"], 2 * b + l + 1)
                for slot_ in range(2):
                    hs = slice(8 * slot_, 8 * slot_ + 8)
                    dve.tensor_tensor(
                        vst[:, :, hs, 8 * slot_:8 * slot_ + 8],
                        SC[:, 1, 0:S].rearrange("p (k h d) -> p k h d", k=2, d=HD)[:, :, hs],
                        c("bv")[:, 128 * l:128 * l + 128].rearrange("p (o h d) -> p o h d", o=1, d=HD)[:, :, hs].to_broadcast([128, 2, 8, HD]),
                        ALU.add).then_inc(s["v_sb"], 1)
                dve.wait_ge(s["q_hi"], 2 * b + l + 1)
                dve.scalar_tensor_tensor(ql[:], SC[:, 2, 0:S], c("bq")[:, l:l + 1], qh[:].bitcast(F32),
                                         ALU.add, ALU.subtract).then_inc(s["q_lo"], 1)

            def stacks(b, l):
                for half, bank in ((0, 2), (1, 1)):
                    dve.wait_ge(s["qstack_ps"], 4 * b + 2 * l + half + 1)
                    dve.tensor_scalar(qs[:, 2 * half:2 * half + 2].rearrange("p t q -> p (t q)"), SC[:, bank],
                                      c("qaux"), None, ALU.add).then_inc(s["qstack_sb"], 1)

            def maxima(b, l):
                for n in range(8):
                    qt, tp, u = unit(n)
                    dve.wait_ge(s["s_ps"], 16 * b + 8 * l + n + 1)
                    scores = SC[:, 2 * u:2 * u + 2].rearrange("p i (t k) -> p i t k", t=2)
                    if l == 1:
                        parts = [(0, 128, 0, 256)]
                    elif qt == 0:
                        parts = [(0, 64, 0, 64), (64, 128, 64, 128)]
                    else:
                        parts = [(0, 64, 0, 256), (64, 128, 192, 256)]
                    for p0, p1, k0, k1 in parts:
                        last = dve.tensor_reduce(mx[p0:p1, qt, 2 * u:2 * u + 2, 2 * tp:2 * tp + 2],
                                                 scores[p0:p1, :, :, k0:k1], AX, ALU.max)
                    last.then_inc(s["s_max"], 1)

            def normalize(b, l, done, settle):
                wait_apart(dve, s["pv_ps"], 4 * b + 2 * l + 2)
                done(dve.stream_shuffle(sh[:], PV[:], [16 + r % 16 for r in range(32)]))
                settle()
                done(dve.reciprocal(rsh[:], sh[:]))
                settle()
                dve.tensor_tensor(on[:].rearrange("p a q -> p (a q)"), PV[:], rsh[:], ALU.mult).then_inc(s["on_sb"], 1)

            def residual(b, l, src, dst):
                dve.wait_ge(s["y_ps"], 2 * b + l + 1)
                if l == 1 and not first_of(b):
                    dve.wait_ge(s["xb3_sb"], b)
                dve.scalar_tensor_tensor(dst[:], SC[:, 0, 0:S].rearrange("p (q d) -> p q d", q=2), gate[:, 2 * l:2 * l + 1],
                                         src[:], ALU.mult, ALU.add).then_inc(s["x_res"], 1)

            def ffn(b, done, settle):
                dve.wait_ge(s["xn_sb"], 4 * b + 2)
                quantize(dve, done, settle, xn[:].rearrange("p q (n k) -> p (q n) k", k=32), 2 * NB, xd[:], s["xd_sb"])

            def ffn_residual(b):
                dve.wait_ge(s["ffn_ps"], b + 1)
                dve.wait_ge(s["x1b_sb"], b + 1)
                dve.scalar_tensor_tensor(x2[:], SC[:, 2, 0:S].rearrange("p (q d) -> p q d", q=2), gate[:, 1:2],
                                         x1b[:], ALU.mult, ALU.add).then_inc(s["x_res"], 1)

            def router(m, done, settle):
                dve.wait_ge(s["logits_ps"], m + 1)
                done(dve.tensor_tensor(lg[:], OP[:, 0:2 * E].rearrange("p (q e) -> p q e", q=2),
                                       c("br").unsqueeze(1).to_broadcast([128, 2, E]), ALU.add))
                settle(apart=True)
                for qt in range(2):
                    done(dve.max(top[:, qt], lg[:, qt]))
                settle()
                dve.tensor_tensor(gap[:], top[:, :, 1:2], top[:, :, 0:1], ALU.subtract).then_inc(s["gap_sb"], 1)
                for qt in range(2):
                    done(dve.max_index(topi[:, qt], top[:, qt], lg[:, qt]))
                settle()
                done(dve.tensor_copy(topf[:], topi[:]))

            def router_weights(m, done, settle):
                dve.wait_ge(s["egap_sb"], m + 1)
                done(dve.tensor_scalar(den[:], egap[:], 1.0, None, ALU.add))
                settle()
                done(dve.reciprocal(tw[:, :, 0:1], den[:]))
                settle()
                done(dve.tensor_tensor(tw[:, :, 1:2], egap[:], tw[:, :, 0:1], ALU.mult))
                settle()
                for qt in range(2):
                    dve.tensor_scalar(r1[:, qt], c("iota"), topf[:, qt, 0:1], tw[:, qt, 0:1], ALU.is_equal, ALU.mult)
                    last = dve.tensor_scalar(r2[:, qt], c("iota"), topf[:, qt, 1:2], tw[:, qt, 1:2], ALU.is_equal, ALU.mult)
                done(last)
                settle()
                done(dve.tensor_tensor(rw[:], r1[:], r2[:], ALU.add))
                settle()
                done(dve.tensor_copy(wc[:, :, 0:E], rw[:]))
                settle()
                dve.tensor_tensor(wc[:, :, E:2 * E], rw[:], wc[:, :, 0:E].bitcast(F32), ALU.subtract).then_inc(s["weights_sb"], 1)

            def slot(m, n):
                if n >= 1:
                    e = n - 1
                    dve.wait_ge(s["o_ps"], E * m + e + 1)
                    if e >= 2:
                        dve.wait_ge(s["acc_sb"], E * m + e - 1)
                    dve.scalar_tensor_tensor(te[:, e % 2], OP[:, 0:S], c("b2")[:, e:e + 1], wbc[:, e],
                                             ALU.add, ALU.mult).then_inc(s["te_sb"], 1)

            def moe_out(m, done, settle):
                dve.wait_ge(s["zT_ps"], m + 1)
                for qt in range(2):
                    done(dve.bn_stats(zst[:, qt], OP[:, qt * 128:qt * 128 + 128]))
                settle(apart=True)
                for qt in range(2):
                    last = dve.bn_aggr(zmv[:, qt], zst[:, qt])
                last.then_inc(s["z_stats"], 1)
                dve.wait_ge(s["z_rstd"], m + 1)
                for qt in range(2):
                    last = dve.tensor_scalar(zn[:, qt], OP[:, qt * 128:qt * 128 + 128], zmv[:, qt, 0:1], zrs[:, qt:qt + 1],
                                             ALU.subtract, ALU.mult)
                last.then_inc(s["zn_sb"], 1)

            def both(b, m):
                a_done, a_settle, a_n = counted(dve, s["attn_step"], b * ATTN_STEPS) if b is not None else (None,) * 3
                z_done, z_settle, z_n = counted(dve, s["moe_step"], m * MOE_STEPS) if m is not None else (None,) * 3
                if b is not None:
                    dve.wait_ge(s["x_in"], 16 * b + 16)
                    layer_norm(xin, 4 * b + 1, a_done, a_settle)
                if m is not None:
                    router(m, z_done, z_settle)
                if b is not None:
                    front(b, 0)
                if m is not None:
                    router_weights(m, z_done, z_settle)
                if b is not None:
                    stacks(b, 0)
                    maxima(b, 0)
                if m is not None:
                    slot(m, 1)
                    slot(m, 2)
                if b is not None:
                    normalize(b, 0, a_done, a_settle)
                    residual(b, 0, xin, x1)
                    dve.wait_ge(s["x_res"], 3 * b + 1)
                    layer_norm(x1, 4 * b + 2, a_done, a_settle)
                if m is not None:
                    slot(m, 3)
                if b is not None:
                    ffn(b, a_done, a_settle)
                if m is not None:
                    slot(m, 4)
                    slot(m, 5)
                if b is not None:
                    ffn_residual(b)
                    batch_bias(b)
                    dve.wait_ge(s["x_res"], 3 * b + 2)
                    layer_norm(x2, 4 * b + 3, a_done, a_settle)
                if m is not None:
                    slot(m, 6)
                if b is not None:
                    front(b, 1)
                if m is not None:
                    slot(m, 7)
                if b is not None:
                    stacks(b, 1)
                    maxima(b, 1)
                if m is not None:
                    slot(m, 8)
                    moe_out(m, z_done, z_settle)
                if b is not None:
                    normalize(b, 1, a_done, a_settle)
                    residual(b, 1, x2, x3)
                    dve.wait_ge(s["x_res"], 3 * b + 3)
                    if not first_of(b):
                        dve.wait_ge(s["x3T_ps"], b)
                    layer_norm(x3, 4 * b + 4, a_done, a_settle, x3n)
                assert a_n is None or a_n[0] == ATTN_STEPS, a_n
                assert z_n is None or z_n[0] == MOE_STEPS, z_n

            dve.wait_ge(s["const_in"], 16)
            dve.tensor_copy(rnd[:], cst[:, 0:N_ROUNDED]).then_inc(s["rounded"], 1)
            p_done, p_settle, _ = counted(dve, s["prep_step"], 0)
            dve.wait_ge(s["side_in"], 64)
            for side, mask, kb, keep, pen in ((sidec, maskc, kbc, keepc, penc), (sider, maskr, kbr, keepr, penr)):
                p_done(dve.scalar_tensor_tensor(keep[:], side[:], 1.0 / SCALE, mask[:], ALU.mult, ALU.mult))
                p_done(dve.tensor_scalar(pen[:], mask[:], -1.0, FAR, ALU.add, ALU.mult))
                p_settle()
                p_done(dve.tensor_tensor(kb[:], keep[:], pen[:], ALU.add))
                p_settle()
            p_done(dve.tensor_scalar(penc[:], maskc[:], -1.0, 3e38, ALU.add, ALU.mult))
            p_done(dve.scalar_tensor_tensor(keepc[:], kbc[:].bitcast(F32), -SCALE, sidec[:], ALU.mult, ALU.add))
            p_settle()
            p_done(dve.tensor_tensor(ebc[:], keepc[:], penc[:], ALU.add))
            p_settle()
            dve.wait_ge(s["ffn_w_in"], 16)
            quantize(dve, p_done, p_settle, wfr[:].rearrange("p (n k) -> p n k", k=32), NB,
                     wdq[:].rearrange("p (n k) -> p n k", k=32), s["wd_quant"])
            dve.wait_ge(s["gates_done"], 1)
            dve.wait_ge(s["wd_quant"], 1)
            both(0, None)
            with dve.Fori(0, B - 1) as m:
                both(m + 1, m)
            both(None, B - 1)

        @block.gpsimd
        def _(pool):
            def rstd_of(done_sem, veps_sem, rstd_sem, k, mv_, ve, rs):
                wait_apart(pool, done_sem, k)
                pool.tensor_scalar(ve[:].unsqueeze(2), mv_[:, :, 1:2], EPS, None, ALU.add).then_inc(veps_sem, 1)
                pool.wait_ge(veps_sem, k)
                pool.tensor_tensor(rs[:], ve[:], halfs[:], ALU.pow).then_inc(rstd_sem, 1)

            def ln(k):
                rstd_of(s["ln_stats"], s["ln_veps"], s["ln_rstd"], k, mv, veps, rstd)

            def mask_out(b):
                for n in range(8):
                    tp, kt, u = unit(n)
                    wait_apart(pool, s["exp_sb"], 16 * b + n + 1)
                    hs = 2 * tp + u

                    def keep(rows, kt_, q0, per_q, per_key, base):
                        blk = P[0:rows, kt_, hs, :, q0:q0 + 64]
                        pool.affine_select(out=blk, in_=blk, pattern=[[0, 4], [per_q, 64]], compare_op=ALU.is_ge, fill=0.0,
                                           base=base, channel_multiplier=per_key).then_inc(s["p_masked"], 1)
                    if kt == 0:
                        keep(128, 0, 0, 0, -1, 63)
                        keep(128, 0, 64, 0, 1, -64)
                    else:
                        keep(128, 1, 192, 0, 1, -64)
                        keep(64, 1, 128, 1, -1, 0)

            def x1_bias(b):
                pool.wait_ge(s["x_res"], 3 * b + 1)
                pool.tensor_tensor(x1b[:], x1[:], gfb[:].unsqueeze(1).to_broadcast([128, 2, D]), ALU.add).then_inc(s["x1b_sb"], 1)

            def x3_bias(m):
                pool.wait_ge(s["x_res"], 3 * m + 3)
                pool.wait_ge(s["out_sb"], m + 1)
                pool.tensor_tensor(xb3[:], x3[:], gbet[:].unsqueeze(1).to_broadcast([128, 2, D]), ALU.add).then_inc(s["xb3_sb"], 1)

            def slot(m, n):
                if n >= 1:
                    e = n - 1
                    pool.wait_ge(s["te_sb"], E * m + e + 1)
                    if e == 0:
                        pool.wait_ge(s["x3T_sb"], m + 1)
                    else:
                        pool.wait_ge(s["acc_sb"], E * m + e)
                    pool.tensor_tensor(acc[:], x3T[:] if e == 0 else acc[:], te[:, e % 2], ALU.add).then_inc(s["acc_sb"], 1)

            def moe_out(m):
                rstd_of(s["z_stats"], s["z_veps"], s["z_rstd"], m + 1, zmv, zve, zrs)
                pool.wait_ge(s["zn_sb"], m + 1)
                pool.tensor_tensor(zg[:], zn[:], ggam[:].unsqueeze(1).to_broadcast([128, 2, D]), ALU.mult).then_inc(s["pool_prep"], 1)
                pool.wait_ge(s["pool_prep"], 5 + m + 1)
                pool.wait_ge(s["stored"], 16 * m + 16)
                pool.tensor_tensor(outt[:], zg[:], xb3[:], ALU.add).then_inc(s["out_sb"], 1)

            def both(b, m):
                if b is not None:
                    ln(4 * b + 1)
                if m is not None:
                    x3_bias(m)
                    slot(m, 1)
                if b is not None:
                    mask_out(b)
                if m is not None:
                    slot(m, 2)
                if b is not None:
                    x1_bias(b)
                    ln(4 * b + 2)
                if m is not None:
                    for n in (3, 4, 5):
                        slot(m, n)
                if b is not None:
                    ln(4 * b + 3)
                if m is not None:
                    for n in (6, 7, 8):
                        slot(m, n)
                    moe_out(m)
                if b is not None:
                    ln(4 * b + 4)

            pool.memset(halfs[:], -0.5).then_inc(s["pool_prep"], 1)
            pool.memset(vst[:], 0.0).then_inc(s["pool_prep"], 1)
            pool.wait_ge(s["pool_prep"], 2)
            pool.memset(vst[:, :, 0:8, 16:24], 1.0).then_inc(s["ones_set"], 1)
            pool.memset(vst[:, :, 8:16, 24:32], 1.0).then_inc(s["ones_set"], 1)
            pool.memset(outt[:], 0.0).then_inc(s["out_sb"], 1)
            pool.wait_ge(s["gates_done"], 1)
            for src, dst, g in (("ffn_b", gfb, 1), ("gamma", ggam, 3), ("beta", gbet, 3)):
                pool.tensor_scalar(dst[:], c(src), gate[:, g:g + 1], None, ALU.mult).then_inc(s["pool_prep"], 1)
            pool.wait_ge(s["pool_prep"], 5)
            both(0, None)
            with pool.Fori(0, B - 1) as m:
                both(m + 1, m)
            both(None, B - 1)


ORDER = np.concatenate([np.arange(0, 128), np.arange(192, 256), np.arange(128, 192)])


def head_of(tile, j, slot_):
    i, t = 2 * slot_ + j // 2, 2 * tile + j % 2
    return 4 * i + t


def tokens(a):
    return np.ascontiguousarray(a[:, ORDER].reshape(B, 2, 128, D).transpose(2, 0, 1, 3))


def constants(v):
    cst = np.zeros((128, NCONST), np.float32)

    def put(name, a):
        lo, hi = CONST_AT[name]
        a = np.asarray(a, np.float32)
        cst[0:a.shape[0], lo:hi] = a.reshape(a.shape[0], hi - lo)
    put("ident", np.eye(128))
    sel = np.zeros((128, 4, 4, 128), np.float32)
    for t in range(4):
        for i in range(4):
            for d in range(HD):
                ch, row = HD * (4 * i + t) + d, 32 * i + d
                for kind, rows in ((0, (0, 16)), (1, (8,)), (2, (0, 8)), (3, (16,))):
                    for r in rows:
                        sel[ch, kind, t, row + r] = 1
    put("sel", sel)
    aux = np.zeros((1, 128))
    aux[0, ROW_BIAS::32] = 1
    put("auxsel", aux)
    causal = np.zeros((128, 64))
    causal[0:64] = np.where(np.arange(64)[None] > np.arange(64)[:, None], -FAR, 0)
    put("causal", causal)
    wsel = np.zeros((2 * E, E, 128))
    for e in range(E):
        wsel[e, e] = wsel[E + e, e] = 1
    put("wsel", wsel)
    qaux, kaux = np.zeros((128, 1)), np.zeros((128, 1))
    qaux[ROW_BIAS::32] = 1
    kaux[ROW_MAX::32] = 1
    put("qaux", qaux)
    put("kaux", kaux)
    put("iota", np.tile(np.arange(E), (128, 1)))
    put("b1", v["L1_ffn_b1"].reshape(E * FB, 128).T)
    put("b2", v["L1_ffn_b2"].T)
    put("bq", np.stack([v["L0_xattn_bq"], v["L1_xattn_Wq_b"]], 1))
    put("bk", np.stack([v["L0_xattn_bk"], v["L1_xattn_Wkv_b"][0:D]], 1))
    g = [v["g_xattn"][0], v["g_ffn"][0], v["g_xattn"][1], v["g_ffn"][1]]
    for name, row in (("gates", g), ("bv", np.concatenate([v["L0_xattn_bv"], v["L1_xattn_Wkv_b"][D:]])),
                      ("ffn_b", v["L0_ffn_bias"]), ("gamma", v["L1_ffn_gamma"]), ("beta", v["L1_ffn_beta"]),
                      ("br", v["L1_ffn_br"])):
        put(name, np.broadcast_to(np.asarray(row)[None], (128, len(row))))
    return cst


def out_weight(w, b):
    o = np.zeros((128, 2, D), np.float32)
    for tile in range(2):
        for j in range(4):
            for slot_ in range(2):
                h, r = head_of(tile, j, slot_), 32 * j + 8 * slot_
                o[r:r + HD, tile] = w[HD * h:HD * h + HD]
    o[16, 0] = b
    return o


def kernel(**inputs):
    import concourse.bacc as bacc
    from concourse.bass_utils import run_bass_kernel_spmd

    v = {k: np.asarray(a) for k, a in inputs.items()}
    side, mask = v["fside_BxS2_0"][:, ORDER], v["mask_BxS2_bk0"][:, ORDER]
    wkv = v["L1_xattn_Wkv_w"]
    w_attn = np.zeros((128, 2, 5, D), np.float32)
    w_attn[:, 0, 0], w_attn[:, 0, 1], w_attn[:, 0, 2] = v["L0_xattn_Wq"], v["L0_xattn_Wk"], v["L0_xattn_Wv"]
    w_attn[:, 1, 0], w_attn[:, 1, 1], w_attn[:, 1, 2] = v["L1_xattn_Wq_w"].T, wkv[0:D].T, wkv[D:].T
    w_attn[:, 0, 3:] = out_weight(v["L0_xattn_Wo"], v["L0_xattn_bo"])
    w_attn[:, 1, 3:] = out_weight(v["L1_xattn_out_w"].T, v["L1_xattn_out_b"])
    arrays = {
        "x": tokens(v["x"]), "ctx": tokens(v["ctx_1024"]),
        "side_col": side.reshape(B, 2, 128).transpose(2, 0, 1), "mask_col": mask.reshape(B, 2, 128).transpose(2, 0, 1),
        "side_row": side.reshape(1, B * S), "mask_row": mask.reshape(1, B * S),
        "const": constants(v), "w_attn": w_attn, "w_ffn": v["L0_ffn_weight"], "w_router": v["L1_ffn_Wr"].T,
        "w1": v["L1_ffn_W1"].reshape(E * FB, 128, D).transpose(2, 0, 1),
        "w2": v["L1_ffn_W2"].reshape(E, D, FB, 128).transpose(3, 0, 2, 1).reshape(128, E * FB, D),
    }
    arrays = {f"in_{k}": np.ascontiguousarray(a) for k, a in arrays.items()}
    nc = bacc.Bacc("TRN2", target_bir_lowering=False, num_devices=1)
    args = [nc.dram_tensor(k, a.shape, mybir.dt.from_np(a.dtype), kind="ExternalInput").ap() for k, a in arrays.items()]
    args.append(nc.dram_tensor("out_0", (128, B, 2, D), F32, kind="ExternalOutput").ap())
    program(nc, *args)
    got = run_bass_kernel_spmd(nc, [arrays], core_ids=[0]).results[0]["out_0"]
    back = np.argsort(ORDER)
    return np.ascontiguousarray(got.transpose(1, 2, 0, 3).reshape(B, S, D)[:, back])
```

```python
import numpy as np
import concourse.bass as bass
from concourse import mybir
from contextlib import ExitStack

F32 = mybir.dt.float32
F32R = mybir.dt.float32r
I32 = mybir.dt.int32
U32 = mybir.dt.uint32
U8 = mybir.dt.uint8
ALU = mybir.AluOpType
ACT = mybir.ActivationFunctionType
AX = mybir.AxisListType.X

B, S, D, H, E, F = 8, 256, 128, 16, 8, 512
HD = D // H
NB = D // 32
FB = F // 128
SCALE = HD ** -0.5
FAR = 1e30
EPS = 1e-5
ROW_MAX, ROW_BIAS = 24, 25

def columns(widths):
    at, n = {}, 0
    for name, w in widths:
        at[name] = (n, n + w)
        n += w
    return at, n


CONST_AT, NCONST = columns([("ident", 128), ("qaux", 1), ("kaux", 1), ("iota", E), ("b1", E * FB), ("b2", E), ("bq", 2),
                            ("bk", 2), ("gates", 4), ("bv", 2 * 128), ("ffn_b", 128), ("gamma", 128), ("beta", 128),
                            ("br", E)])
SEL_AT, NSEL = columns([("sel", 4 * 4 * 128), ("auxsel", 128), ("eye", 128), ("causal", 64), ("wsel", E * 128)])


def program(nc, x, ctx_in, side_col, mask_col, side_row, mask_row, const, selectors, w_attn, w_ffn, w_router, w1, w2, out):
    stack = ExitStack()
    with stack:
        def sb(name, shape, dt=F32):
            return stack.enter_context(nc.sbuf_tensor(name, shape, dt))

        def sem(name):
            return stack.enter_context(nc.semaphore(name))

        cst = sb("cst", [128, NCONST])
        rnd = sb("rnd", [128, NSEL], F32R)

        def c(name):
            a, b = CONST_AT[name]
            return cst[:, a:b]

        def cr(name):
            a, b = SEL_AT[name]
            return rnd[:, a:b]

        ident = c("ident")
        sel = cr("sel").rearrange("p (k t m) -> p k t m", k=4, t=4)
        wsel = cr("wsel").rearrange("p (e m) -> p e m", e=E)
        wat = sb("wat", [128, 2, 5, 128])
        wfr = sb("wfr", [128, 128])
        wdq = sb("wdq", [128, 128])
        wdT = sb("wdT", [128, 128])
        wrT = sb("wrT", [128, E])
        w1s = sb("w1s", [128, E * FB, 128])
        w2s = sb("w2s", [128, E * FB, 128])
        gate = sb("gate", [128, 4])
        gfb = sb("gfb", [128, 128])
        ggam = sb("ggam", [128, 128])
        gbet = sb("gbet", [128, 128])
        halfs = sb("halfs", [128, 2])
        sidec = sb("sidec", [128, B, 2])
        maskc = sb("maskc", [128, B, 2], U8)
        keepc = sb("keepc", [128, B, 2])
        penc = sb("penc", [128, B, 2])
        kbc = sb("kbc", [128, B, 2], F32R)
        ebc = sb("ebc", [128, B, 2])
        ebias = sb("ebias", [128, 2])
        sider = sb("sider", [B, S])
        maskr = sb("maskr", [B, S], U8)
        keepr = sb("keepr", [B, S])
        penr = sb("penr", [B, S])
        kbb = sb("kbb", [B, S], F32R)
        kbr = sb("kbr", [1, B * S], F32R)
        kbrow = sb("kbrow", [1, S], F32R)

        xin = sb("xin", [128, 2, D])
        xres = sb("xres", [128, 2, D])
        cin = sb("cin", [128, 2, D])
        x1 = sb("x1", [128, 2, D])
        x1b = sb("x1b", [128, 2, D])
        x2 = sb("x2", [128, 2, D])
        x3 = sb("x3", [128, 2, D])
        x3n = sb("x3n", [128, 2, D])
        stats, mv, veps, rstd = ({n: sb(f"{what}_{n}", shape) for n in ("lnx", "lnf", "lny", "lnz")} for what, shape in
                                 (("stats", [128, 2, 6]), ("mv", [128, 2, 2]), ("veps", [128, 2]), ("rstd", [128, 2])))
        def two(name, shape, dt=F32):
            return [sb(f"{name}{l}", shape, dt) for l in range(2)]
        xn = two("xn", [128, 2, D])
        xnT = two("xnT", [128, S])
        ctxT = two("ctxT", [128, S])
        qh = two("qh", [128, S], F32R)
        ql = two("ql", [128, S], F32R)
        kh = two("kh", [128, S], F32R)
        kl = two("kl", [128, S], F32R)
        qs = two("qs", [128, 4, S], F32R)
        ks = two("ks", [128, 4, S], F32R)
        vst = two("vst", [128, 2, H, 32])
        mx = two("mx", [128, 2, 4, 4])
        mneg = two("mneg", [H, S], F32R)
        P = sb("P", [128, 2, 4, 4, S])
        pvs = sb("pvs", [128, 2 * S])
        sh = sb("sh", [128, 2 * S])
        rsh = sb("rsh", [128, 2 * S])
        sel_raw = P[:].rearrange("p a b c q -> p (a b c q)")[:, 0:NSEL]
        on = two("on", [128, 2, S])
        xf = sb("xf", [128, 2, D])
        bmax = sb("bmax", [128, 2 * NB])
        scl = sb("scl", [128, 2 * NB])
        rscl = sb("rscl", [128, 2 * NB])
        yq = sb("yq", [128, 2 * NB, 32])
        eb = sb("eb", [128, 2 * NB, 32], I32)
        ib = sb("ib", [128, 2 * NB, 32], I32)
        rq = sb("rq", [128, 2 * NB, 32])
        ps_ = sb("ps_", [128, 2 * NB, 32])
        xd = sb("xd", [128, 2 * NB, 32])
        xdT = sb("xdT", [128, S])
        x3T = sb("x3T", [128, S])
        xb3 = sb("xb3", [128, 2, D])
        lg = sb("lg", [128, 2, E])
        top = sb("top", [128, 2, 8])
        topi = sb("topi", [128, 2, 8], U32)
        topf = sb("topf", [128, 2, 8])
        gap = sb("gap", [128, 2, 1])
        egap = sb("egap", [128, 2, 1])
        den = sb("den", [128, 2, 1])
        tw = sb("tw", [128, 2, 2])
        r1 = sb("r1", [128, 2, E])
        r2 = sb("r2", [128, 2, E])
        rw = sb("rw", [128, 2, E])
        wc = sb("wc", [128, 2, 2 * E], F32R)
        wT = sb("wT", [2 * E, S], F32R)
        wbc = sb("wbc", [128, E, S])
        hbuf = sb("hbuf", [128, 2, FB, S])
        te = sb("te", [128, 2, S])
        acc = sb("acc", [128, S])
        zst = sb("zst", [128, 2, 6])
        zmv = sb("zmv", [128, 2, 2])
        zve = sb("zve", [128, 2])
        zrs = sb("zrs", [128, 2])
        zn = sb("zn", [128, 2, D])
        zg = sb("zg", [128, 2, D])
        outt = sb("outt", [128, 2, D])

        SC = stack.enter_context(nc.psum_tensor("SC", [128, 4, 512], F32))
        PV = stack.enter_context(nc.psum_tensor("PV", [128, 512], F32))
        HP = stack.enter_context(nc.psum_tensor("HP", [128, 2, 512], F32))
        OP = stack.enter_context(nc.psum_tensor("OP", [128, 512], F32))

        names = """apart const_in sel_in bias_rows bias_row_in attn0_w_in attn1_w_in ffn_w_in router_w_in w1_in w2_in side_in x_in ctx_in_ xres_sb rounded ones_set
            gates_done prep_step pool_prep wd_quant wdT_ps wdT_sb batch_bias
            lnx_stats lnx_veps lnx_rstd lnf_stats lnf_veps lnf_rstd lny_stats lny_veps lny_rstd lnz_stats lnz_veps lnz_rstd
            xf_sb x3n_sb ctxT_ps ctx0_sb ctx1_sb p_masked pvs_sb x1_sb x2_sb x3_sb x1b_sb xd_sb xdT_ps xdT_sb ffn_ps
            next_step attn0_step attn1_step x3T_ps x3T_sb xb3_sb logits_ps gap_sb egap_sb weights_sb wT_ps wT_sb wbc_ps wbc_sb
            h_ps relu_sb o_ps te_sb acc_sb zT_ps z_stats z_veps z_rstd zn_sb zg_sb out_sb stored moe_step""".split()
        s = {n: sem(n) for n in names}
        for n in """xn_sb k_ps v_ps xnT_ps xnT_sb q_ps k_hi q_hi k_lo q_lo v_sb kstack_ps qstack_ps kstack_sb qstack_sb
                s_ps s_max mxT_ps mneg_sb max_row st_ps exp_sb pv_ps on_sb y_ps""".split():
            s[n] = [sem(f"{n}{l}") for l in range(2)]

        NEXT_STEPS, ATTN0_STEPS, ATTN1_STEPS, MOE_STEPS = 2, 18, 4, 14

        S0_STEPS = ((), (), (0,), (2,), (4,), (5,), (6,), (7, 8))
        MID_STEPS = ((9,), (10,), (11,), (12, 13))
        S1_STEPS = ((14,), (15,), (), (16,), (17,), (), (18,), (19,))
        A0_STEPS = ((20,), (), (21,), (), (22,), (), (23,), ())
        A1_STEPS = ((), (24,), (), (26,), (), (), (), (25,))
        TAIL_STEPS = ((27,), (28,), (29,), (30,), (31,), (33,), (35,))
        PROJECT_AT, PROJECT_STEP = 5, 23

        def first_of(b):
            return isinstance(b, int) and b == 0

        def counted(eng, semaphore, base):
            n = [0]

            def done(ins):
                n[0] += 1
                return ins.then_inc(semaphore, 1)

            def settle(apart=False):
                (wait_apart(eng, semaphore, base + n[0]) if apart else eng.wait_ge(semaphore, base + n[0]))
            return done, settle, n

        def wait_apart(eng, semaphore, value):
            eng.wait_ge(semaphore, value)
            if not isinstance(value, int):
                eng.sem_inc(s["apart"])

        def quantize(dve, done, settle, src, nb, dst, last=None):
            def bc(t):
                return t[:, 0:nb].unsqueeze(2).to_broadcast([128, nb, 32])
            v = slice(0, nb)
            done(dve.tensor_reduce(bmax[:, v], src, AX, ALU.max, apply_absolute_value=True))
            settle()
            done(dve.tensor_scalar(scl[:, v], bmax[:, v], 1.0 / 7.5, 1e-30, ALU.mult, ALU.max))
            settle()
            done(dve.reciprocal(rscl[:, v], scl[:, v]))
            settle()
            done(dve.tensor_tensor(yq[:, v], src, bc(rscl), ALU.mult))
            settle()
            done(dve.tensor_scalar(eb[:, v], yq[:, v].bitcast(I32), 0x7F800000, None, ALU.bitwise_and))
            settle()
            done(dve.tensor_scalar(eb[:, v].bitcast(F32), eb[:, v].bitcast(F32), 1.0, 4.0, ALU.max, ALU.min))
            settle()
            done(dve.tensor_scalar(ib[:, v], eb[:, v], -1.0, float(257 << 23), ALU.mult, ALU.add))
            done(dve.tensor_tensor(ps_[:, v], eb[:, v].bitcast(F32), bc(scl), ALU.mult))
            settle()
            done(dve.tensor_tensor(yq[:, v], yq[:, v], ib[:, v].bitcast(F32), ALU.mult))
            settle()
            done(dve.tensor_scalar(rq[:, v], yq[:, v], 12582912.0, -12582912.0, ALU.add, ALU.add))
            settle()
            done(dve.tensor_tensor(yq[:, v], rq[:, v], yq[:, v], ALU.subtract))
            settle()
            done(dve.scalar_tensor_tensor(yq[:, v], yq[:, v], 0.5, rq[:, v], ALU.is_ge, ALU.subtract))
            settle()
            ins = dve.scalar_tensor_tensor(dst, yq[:, v], -0.125, ps_[:, v], ALU.mult, ALU.mult)
            (ins.then_inc(last, 1) if last is not None else done(ins))

        def q_range(l, kt):
            return (0, S) if l == 1 else ((0, 192), (128, 256))[kt]

        def unit(n):
            return n // 4, (n // 2) % 2, n % 2

        def flat(t):
            return t[:].rearrange("p q d -> p (q d)")

        def stages(enter, body, loop):
            enter(0)
            body(0, None, None, 1)
            body(1, 0, None, 2)
            with loop(0, B - 3) as m:
                body(m + 2, m + 1, m, m + 3)
            body(B - 1, B - 2, B - 3, None)
            body(None, B - 1, B - 2, None)
            body(None, None, B - 1, None)

        block = stack.enter_context(nc.Block())

        @block.sync
        def _(sp):
            def load(b):
                sp.dma_start(xin[:], x[:, bass.ds(b, 1)].rearrange("p o q d -> p (o q) d")).then_inc(s["x_in"], 16)
                sp.dma_start(cin[:], ctx_in[:, bass.ds(b, 1)].rearrange("p o q d -> p (o q) d")).then_inc(s["ctx_in_"], 16)

            def max_rows(b, l):
                sp.wait_ge(s["mneg_sb"][l], b + 1)
                for i in range(4):
                    r = 32 * i + ROW_MAX
                    sp.dma_start(qs[l][r:r + 1, :, :].bitcast(F32),
                                 mneg[l][4 * i:4 * i + 4, :].bitcast(F32)).then_inc(s["max_row"][l], 16)

            def store(m):
                wait_apart(sp, s["out_sb"], m + 2)
                sp.dma_start(out[:, bass.ds(m, 1)].rearrange("p o q d -> p (o q) d"), outt[:]).then_inc(s["stored"], 16)

            def body(b0, b1, m, nxt):
                if nxt is not None:
                    sp.wait_ge(s["ctxT_ps"], b0 + 1)
                    sp.wait_ge(s["xn_sb"][0], b0 + 1)
                    wait_apart(sp, s["xres_sb"], b0 + 1)
                    load(nxt)
                if b0 is not None:
                    max_rows(b0, 0)
                if b1 is not None:
                    max_rows(b1, 1)
                if m is not None:
                    store(m)

            sp.sem_inc(s["stored"], 16)
            sp.dma_start(cst[:], const).then_inc(s["const_in"], 16)
            sp.dma_start(wat[:, 0], w_attn[:, 0]).then_inc(s["attn0_w_in"], 16)
            load(0)
            sp.dma_start(sel_raw, selectors).then_inc(s["sel_in"], 16)
            sp.dma_start(wfr[:], w_ffn).then_inc(s["ffn_w_in"], 16)
            for dst, src in ((sidec, side_col), (maskc, mask_col), (sider, side_row), (maskr, mask_row)):
                sp.dma_start(dst[:], src).then_inc(s["side_in"], 16)
            sp.dma_start(wat[:, 1], w_attn[:, 1]).then_inc(s["attn1_w_in"], 16)
            sp.dma_start(wrT[:], w_router).then_inc(s["router_w_in"], 16)
            sp.dma_start(w1s[:], w1).then_inc(s["w1_in"], 16)
            sp.dma_start(w2s[:], w2).then_inc(s["w2_in"], 16)
            sp.wait_ge(s["bias_rows"], 1)
            sp.dma_start(kbr[:].bitcast(F32), kbb[:].bitcast(F32)).then_inc(s["bias_row_in"], 16)
            stages(lambda b: None, body, sp.Fori)
            sp.wait_ge(s["stored"], 16 * B + 16)

        @block.tensor
        def _(pe):
            def transpose2(dst, src):
                for t in range(2):
                    last = pe.transpose(dst[:, t * 128:(t + 1) * 128], src[:, t * 128:(t + 1) * 128], ident)
                return last

            def keys_values(b, l):
                pe.matmul(SC[:, 3, 0:S], wat[:, l, 1], ctxT[l][:], start=True, stop=True).then_inc(s["k_ps"][l], 1)
                for t in range(2):
                    last = pe.matmul(SC[:, 1, t * 128:(t + 1) * 128], ctxT[l][:, t * 128:(t + 1) * 128], wat[:, l, 2],
                                     start=True, stop=True)
                last.then_inc(s["v_ps"][l], 1)

            def turn_ctx(b):
                pe.wait_ge(s["ctx_in_"], 16 * b + 16)
                transpose2(SC[:, 1], flat(cin)).then_inc(s["ctxT_ps"], 1)

            def turn_x(b, l):
                pe.wait_ge(s["xn_sb"][l], b + 1)
                transpose2(SC[:, 0], flat(xn[l])).then_inc(s["xnT_ps"][l], 1)

            def queries(b, l):
                pe.wait_ge(s["xnT_sb"][l], b + 1)
                pe.matmul(SC[:, 2, 0:S], wat[:, l, 0], xnT[l][:], start=True, stop=True).then_inc(s["q_ps"][l], 1)

            def stack_keys(b, l, x2_of):
                if first_of(b) and l == 0:
                    pe.wait_ge(s["rounded"], 1)
                pe.wait_ge(s["k_lo"][l], b + 1)
                if l == 1:
                    pe.wait_ge(s["batch_bias"], 2 * b + 2)
                for half, bank in ((0, 3), (1, 0)):
                    if half == 1 and x2_of is not None:
                        pe.wait_ge(s["x2_sb"], x2_of + 1)
                    for tt in range(2):
                        o = SC[:, bank, tt * S:(tt + 1) * S]
                        t = 2 * half + tt
                        pe.matmul(o, sel[:, 2, t], kh[l][:], start=True, stop=False)
                        last = pe.matmul(o, sel[:, 3, t], kl[l][:], start=False, stop=l == 0)
                        if l == 1:
                            last = pe.matmul(o, cr("auxsel")[0:1, :], kbrow[:], start=False, stop=True)
                    last.then_inc(s["kstack_ps"][l], 1)

            def stack_queries(b, l):
                pe.wait_ge(s["q_lo"][l], b + 1)
                pe.wait_ge(s["v_sb"][l], 2 * b + 2)
                for half, bank in ((0, 2), (1, 1)):
                    for tt in range(2):
                        o = SC[:, bank, tt * S:(tt + 1) * S]
                        t = 2 * half + tt
                        pe.matmul(o, sel[:, 0, t], qh[l][:], start=True, stop=False)
                        last = pe.matmul(o, sel[:, 1, t], ql[l][:], start=False, stop=True)
                    last.then_inc(s["qstack_ps"][l], 1)

            def score_unit(b, l, n):
                if n == 0:
                    pe.wait_ge(s["kstack_sb"][l], 2 * b + 2)
                    pe.wait_ge(s["qstack_sb"][l], 2 * b + 2)
                qt, tp, u = unit(n)
                if n >= 2:
                    pe.wait_ge(s["s_max"][l], 8 * b + n - 1)
                nk = 128 if l == 0 and qt == 0 else S
                for tt in range(2):
                    for i in (2 * u, 2 * u + 1):
                        r = slice(32 * i, 32 * i + 32)
                        masked = l == 0 and qt == 1
                        last = pe.matmul(SC[:, i, tt * S:tt * S + nk], qs[l][r, 2 * tp + tt, qt * 128:qt * 128 + 128],
                                         ks[l][r, 2 * tp + tt, 0:nk], start=True, stop=not masked)
                        if masked:
                            last = pe.matmul(SC[:, i, tt * S + 128:tt * S + 192], cr("eye"), cr("causal"),
                                             start=False, stop=True)
                last.then_inc(s["s_ps"][l], 1)

            def max_out(b, l):
                pe.wait_ge(s["s_max"][l], 8 * b + 8)
                for qt in range(2):
                    last = pe.transpose(PV[0:H, qt * 128:qt * 128 + 128], mx[l][:, qt].rearrange("p i t -> p (i t)"), ident)
                last.then_inc(s["mxT_ps"][l], 1)

            def attend_unit(b, l, n):
                if n == 0:
                    pe.wait_ge(s["max_row"][l], 64 * b + 64)
                tp, kt, u = unit(n)
                if n >= 2:
                    pe.wait_ge(s["exp_sb"][l], 8 * b + n - 1)
                a, z = q_range(l, kt)
                for tt in range(2):
                    for i in (2 * u, 2 * u + 1):
                        r = slice(32 * i, 32 * i + 32)
                        last = pe.matmul(SC[:, i, tt * S:tt * S + z - a], ks[l][r, 2 * tp + tt, kt * 128:kt * 128 + 128],
                                         qs[l][r, 2 * tp + tt, a:z], start=True, stop=True)
                last.then_inc(s["st_ps"][l], 1)

            def weigh(b, l, n):
                tp, kt, u = unit(n)
                if l == 0:
                    pe.wait_ge(s["p_masked"], 16 * b + 2 * n + 2)
                else:
                    pe.wait_ge(s["exp_sb"][1], 8 * b + n + 1)
                parts = [q_range(l, kt)] if l == 1 or kt == 0 else [(128, 192), (192, 256)]
                for tt in range(2):
                    for ii in range(2):
                        i, t, j = 2 * u + ii, 2 * tp + tt, 2 * ii + tt
                        for a, z in parts:
                            last = pe.matmul(PV[32 * j:32 * j + 32, tp * S + a:tp * S + z], vst[l][:, kt, 4 * i + t],
                                             P[:, kt, 2 * tp + u, 2 * ii + tt, a:z], start=(kt == 0 and u == 0),
                                             stop=(kt == 1 and u == 1), skip_group_check=True)
                if n == 7:
                    last.then_inc(s["pv_ps"][l], 1)

            def project(b, l, dst):
                pe.wait_ge(s["on_sb"][l], b + 1)
                for qt in range(2):
                    for ab in range(2):
                        last = pe.matmul(dst[:, qt * 128:qt * 128 + 128], on[l][:, ab, qt * 128:qt * 128 + 128],
                                         wat[:, l, 3 + ab], start=(ab == 0), stop=(ab == 1))
                last.then_inc(s["y_ps"][l], 1)

            def ffn_turn(b):
                pe.wait_ge(s["xd_sb"], b + 1)
                transpose2(SC[:, 0], xd[:].rearrange("p n k -> p (n k)")).then_inc(s["xdT_ps"], 1)

            def ffn_out(b):
                pe.wait_ge(s["xdT_sb"], b + 1)
                for qt in range(2):
                    last = pe.matmul(SC[:, 0, qt * 128:qt * 128 + 128], xdT[:, qt * 128:qt * 128 + 128], wdT[:],
                                     start=True, stop=True)
                last.then_inc(s["ffn_ps"], 1)

            def moe_in(m):
                pe.wait_ge(s["x3n_sb"], m + 1)
                transpose2(HP[:, 0], flat(x3n)).then_inc(s["x3T_ps"], 1)
                pe.wait_ge(s["x3T_sb"], m + 1)
                for qt in range(2):
                    last = pe.matmul(PV[:, qt * E:qt * E + E], x3T[:, qt * 128:qt * 128 + 128], wrT[:],
                                     start=True, stop=True)
                last.then_inc(s["logits_ps"], 1)

            def moe_weights(m, g):
                if g == 0:
                    pe.wait_ge(s["weights_sb"], m + 1)
                    for qt in range(2):
                        last = pe.transpose(PV[0:2 * E, qt * 128:qt * 128 + 128], wc[:, qt].bitcast(F32), ident)
                    last.then_inc(s["wT_ps"], 1)
                    pe.wait_ge(s["wT_sb"], m + 1)
                else:
                    pe.wait_ge(s["wbc_sb"], 4 * m + g)
                for e in (2 * g, 2 * g + 1):
                    last = pe.matmul(PV[:, (e % 2) * S:(e % 2) * S + S], wsel[0:2 * E, e], wT[:], start=True, stop=True)
                last.then_inc(s["wbc_ps"], 1)

            def step(m, g, b0):
                e, p = g // 4, (g % 4) // 2
                if g % 2 == 0 and e < E:
                    if e >= 1:
                        pe.wait_ge(s["relu_sb"], 4 * E * m + 4 * (e - 1) + 2 * p + 2)
                    for k in range(2):
                        last = pe.matmul(HP[:, p, k * S:(k + 1) * S], w1s[:, FB * e + 2 * p + k], x3T[:],
                                         start=True, stop=True)
                    last.then_inc(s["h_ps"], 1)
                if g % 2 == 1 and e >= 1:
                    if p == 0 and e >= 2:
                        pe.wait_ge(s["te_sb"], E * m + e - 1)
                    if e == 1 and p == 0:
                        pe.wait_ge(s["zn_sb"], m + 1)
                    if g == PROJECT_STEP + 2 and b0 is not None:
                        pe.wait_ge(s["x1_sb"], b0 + 1)
                    pe.wait_ge(s["relu_sb"], 4 * E * m + 4 * (e - 1) + 2 * p + 2)
                    for k in (2 * p, 2 * p + 1):
                        last = pe.matmul(OP[:, 0:S], w2s[:, FB * (e - 1) + k], hbuf[:, (e - 1) % 2, k],
                                         start=(k == 0), stop=(k == FB - 1))
                    if p == 1:
                        last.then_inc(s["o_ps"], 1)

            def moe_out(m):
                pe.wait_ge(s["acc_sb"], E * m + E)
                transpose2(OP, acc[:]).then_inc(s["zT_ps"], 1)

            def enter(b):
                turn_ctx(b)
                pe.wait_ge(s["ctx0_sb"], b + 1)
                keys_values(b, 0)
                turn_x(b, 0)
                queries(b, 0)
                stack_keys(b, 0, None)
                stack_queries(b, 0)

            def body(b0, b1, m, nxt):
                def steps(gs):
                    for g in gs if m is not None else ():
                        step(m, g, b0)

                for n in range(8):
                    if b0 is not None:
                        score_unit(b0, 0, n)
                    if m is not None:
                        if n == 1:
                            moe_in(m)
                        if n >= 4:
                            moe_weights(m, n - 4)
                    steps(S0_STEPS[n])
                if b1 is not None:
                    if b0 is not None:
                        pe.wait_ge(s["s_max"][0], 8 * b0 + 8)
                    pe.wait_ge(s["ctx1_sb"], b1 + 1)
                    keys_values(b1, 1)
                    turn_x(b1, 1)
                steps(MID_STEPS[0])
                if b1 is not None:
                    queries(b1, 1)
                steps(MID_STEPS[1])
                if b1 is not None:
                    stack_keys(b1, 1, None)
                steps(MID_STEPS[2])
                if b1 is not None:
                    stack_queries(b1, 1)
                steps(MID_STEPS[3])
                for n in range(8):
                    if b1 is not None:
                        score_unit(b1, 1, n)
                    if n == 1 and b0 is not None:
                        if m is not None:
                            pe.wait_ge(s["wbc_sb"], 4 * m + 4)
                        max_out(b0, 0)
                    steps(S1_STEPS[n])
                if b0 is None and b1 is not None:
                    max_out(b1, 1)
                for n in range(8):
                    if b0 is not None:
                        if n < 2 and b1 is not None:
                            pe.wait_ge(s["s_max"][1], 8 * b1 + 7 + n)
                        attend_unit(b0, 0, n)
                        if n == 1:
                            pe.wait_ge(s["mneg_sb"][0], b0 + 1)
                            if b1 is not None:
                                max_out(b1, 1)
                        if n == 2 and b1 is not None:
                            pe.wait_ge(s["mneg_sb"][1], b1 + 1)
                        if n >= 2:
                            weigh(b0, 0, n - 2)
                    steps(A0_STEPS[n])
                for n in range(8):
                    if b1 is not None:
                        if n < 2 and b0 is not None:
                            pe.wait_ge(s["exp_sb"][0], 8 * b0 + 7 + n)
                        attend_unit(b1, 1, n)
                    if n < 2 and b0 is not None:
                        weigh(b0, 0, 6 + n)
                    if b1 is not None and n >= 2:
                        if n == 2:
                            if b0 is not None:
                                pe.wait_ge(s["pvs_sb"], b0 + 1)
                            else:
                                pe.wait_ge(s["mneg_sb"][1], b1 + 1)
                        weigh(b1, 1, n - 2)
                    if n == PROJECT_AT and b0 is not None:
                        if m is not None:
                            pe.wait_ge(s["te_sb"], E * m + (PROJECT_STEP + 1) // 4 - 1)
                        project(b0, 0, OP[:, S:2 * S])
                    steps(A1_STEPS[n])
                if b1 is not None:
                    weigh(b1, 1, 6)
                if nxt is not None:
                    turn_ctx(nxt)
                steps(TAIL_STEPS[0])
                if b1 is not None:
                    weigh(b1, 1, 7)
                if first_of(b0):
                    pe.wait_ge(s["wd_quant"], 1)
                    pe.transpose(SC[:, 3, 0:128], wdq[:], ident).then_inc(s["wdT_ps"], 1)
                    pe.wait_ge(s["wdT_sb"], 1)
                if nxt is not None:
                    pe.wait_ge(s["ctx0_sb"], nxt + 1)
                    keys_values(nxt, 0)
                steps(TAIL_STEPS[1])
                if nxt is not None:
                    turn_x(nxt, 0)
                steps(TAIL_STEPS[2])
                if nxt is not None:
                    queries(nxt, 0)
                if b0 is not None:
                    ffn_turn(b0)
                steps(TAIL_STEPS[3])
                if b0 is not None:
                    ffn_out(b0)
                steps(TAIL_STEPS[4])
                if b1 is not None:
                    project(b1, 1, PV[:, 0:S])
                steps(TAIL_STEPS[5])
                if nxt is not None:
                    stack_keys(nxt, 0, b0)
                    stack_queries(nxt, 0)
                steps(TAIL_STEPS[6])
                if m is not None:
                    moe_out(m)
                if first_of(b0):
                    pe.wait_ge(s["attn1_w_in"], 16)
                    pe.wait_ge(s["router_w_in"], 16)
                    pe.wait_ge(s["w1_in"], 16)
                    pe.wait_ge(s["w2_in"], 16)

            pe.wait_ge(s["const_in"], 16)
            pe.wait_ge(s["attn0_w_in"], 16)
            stages(enter, body, pe.Fori)

        @block.scalar
        def _(act):
            def ctx_keep(b, b1):
                if b1 is not None:
                    act.wait_ge(s["v_ps"][1], b1 + 1)
                act.activation(ctxT[1][:], ctxT[0][:], ACT.Copy).then_inc(s["ctx1_sb"], 1)

            def ctx_turned(b):
                act.wait_ge(s["ctxT_ps"], b + 1)
                if not first_of(b):
                    act.wait_ge(s["ctx1_sb"], b)
                act.activation(ctxT[0][:], SC[:, 1, 0:S], ACT.Copy).then_inc(s["ctx0_sb"], 1)

            def keys(b, l):
                act.wait_ge(s["k_ps"][l], b + 1)
                act.activation(kh[l][:], SC[:, 3, 0:S], ACT.Identity, bias=c("bk")[:, l:l + 1]).then_inc(s["k_hi"][l], 1)

            def x_turned(b, l):
                act.wait_ge(s["xnT_ps"][l], b + 1)
                act.activation(xnT[l][:], SC[:, 0, 0:S], ACT.Copy).then_inc(s["xnT_sb"][l], 1)

            def queries(b, l):
                act.wait_ge(s["q_ps"][l], b + 1)
                act.activation(qh[l][:], SC[:, 2, 0:S], ACT.Identity, bias=c("bq")[:, l:l + 1]).then_inc(s["q_hi"][l], 1)

            def stacks(b, l):
                for half, bank in ((0, 3), (1, 0)):
                    act.wait_ge(s["kstack_ps"][l], 2 * b + half + 1)
                    act.activation(ks[l][:, 2 * half:2 * half + 2].rearrange("p t k -> p (t k)"), SC[:, bank],
                                   ACT.Identity, bias=c("kaux")).then_inc(s["kstack_sb"][l], 1)

            def max_out(b, l):
                act.wait_ge(s["mxT_ps"][l], b + 1)
                act.activation(mneg[l][:], PV[0:H, 0:S], ACT.Copy, scale=-1.0).then_inc(s["mneg_sb"][l], 1)

            def exp_unit(b, l, n):
                tp, kt, u = unit(n)
                a, z = q_range(l, kt)
                act.wait_ge(s["st_ps"][l], 8 * b + n + 1)
                scores = SC[:, 2 * u:2 * u + 2].rearrange("p i (t q) -> p i t q", t=2)[:, :, :, 0:z - a]
                more = {"bias": ebias[:, kt:kt + 1]} if l == 1 else {}
                act.activation(P[:, kt, 2 * tp + u, :, a:z].rearrange("p (i t) q -> p i t q", i=2), scores, ACT.Exp,
                               scale=SCALE, **more).then_inc(s["exp_sb"][l], 1)

            def step(m, g):
                e, p = g // 4, (g % 4) // 2
                if g % 2 == 0 and e < E:
                    act.wait_ge(s["h_ps"], 2 * E * m + 2 * e + p + 1)
                    if e >= 2 and p == 0:
                        act.wait_ge(s["o_ps"], E * m + e - 1)
                    for k in range(2):
                        f = 2 * p + k
                        act.activation(hbuf[:, e % 2, f], HP[:, p, k * S:(k + 1) * S], ACT.Relu,
                                       bias=c("b1")[:, FB * e + f:FB * e + f + 1]).then_inc(s["relu_sb"], 1)

            def enter(b):
                ctx_turned(b)
                keys(b, 0)
                x_turned(b, 0)
                queries(b, 0)
                stacks(b, 0)

            def body(b0, b1, m, nxt):
                def steps(gs):
                    for g in gs if m is not None else ():
                        step(m, g)

                if b0 is not None:
                    if not first_of(b0):
                        act.wait_ge(s["x1_sb"], b0)
                    act.activation(flat(xres), flat(xin), ACT.Copy).then_inc(s["xres_sb"], 1)
                for n in range(8):
                    if m is not None:
                        if n == 1:
                            act.wait_ge(s["x3T_ps"], m + 1)
                            act.activation(x3T[:], HP[:, 0, 0:S], ACT.Copy).then_inc(s["x3T_sb"], 1)
                        if n == 2:
                            act.wait_ge(s["gap_sb"], m + 1)
                            act.activation(egap[:], gap[:], ACT.Exp).then_inc(s["egap_sb"], 1)
                        if n == 4:
                            act.wait_ge(s["wT_ps"], m + 1)
                            act.activation(wT[:], PV[0:2 * E, 0:S], ACT.Copy).then_inc(s["wT_sb"], 1)
                        if n >= 4:
                            g = n - 4
                            act.wait_ge(s["wbc_ps"], 4 * m + g + 1)
                            act.activation(wbc[:, 2 * g:2 * g + 2].rearrange("p e q -> p (e q)"), PV[:],
                                           ACT.Copy).then_inc(s["wbc_sb"], 1)
                    steps(S0_STEPS[n])
                if b1 is not None:
                    keys(b1, 1)
                    x_turned(b1, 1)
                steps(MID_STEPS[0])
                if b1 is not None:
                    queries(b1, 1)
                steps(MID_STEPS[1])
                if b1 is not None:
                    stacks(b1, 1)
                steps(MID_STEPS[2])
                steps(MID_STEPS[3])
                if b0 is not None:
                    ctx_keep(b0, b1)
                for n in range(8):
                    if n == 1 and b0 is not None:
                        max_out(b0, 0)
                    steps(S1_STEPS[n])
                if b0 is None and b1 is not None:
                    max_out(b1, 1)
                for n in range(8):
                    if b0 is not None:
                        exp_unit(b0, 0, n)
                        if n == 1 and b1 is not None:
                            max_out(b1, 1)
                    steps(A0_STEPS[n])
                for n in range(8):
                    if b1 is not None:
                        exp_unit(b1, 1, n)
                    if n == 1 and b0 is not None:
                        act.wait_ge(s["pv_ps"][0], b0 + 1)
                        act.activation(pvs[:], PV[:], ACT.Copy).then_inc(s["pvs_sb"], 1)
                    steps(A1_STEPS[n])
                if nxt is not None:
                    ctx_turned(nxt)
                steps(TAIL_STEPS[0])
                if first_of(b0):
                    act.wait_ge(s["wdT_ps"], 1)
                    act.activation(wdT[:], SC[:, 3, 0:128], ACT.Copy).then_inc(s["wdT_sb"], 1)
                if nxt is not None:
                    keys(nxt, 0)
                steps(TAIL_STEPS[1])
                if nxt is not None:
                    x_turned(nxt, 0)
                steps(TAIL_STEPS[2])
                if nxt is not None:
                    queries(nxt, 0)
                if b0 is not None:
                    act.wait_ge(s["xdT_ps"], b0 + 1)
                    act.activation(xdT[:], SC[:, 0, 0:S], ACT.Copy).then_inc(s["xdT_sb"], 1)
                steps(TAIL_STEPS[3])
                steps(TAIL_STEPS[4])
                steps(TAIL_STEPS[5])
                if nxt is not None:
                    stacks(nxt, 0)
                steps(TAIL_STEPS[6])

            act.wait_ge(s["const_in"], 16)
            act.activation(gate[:], c("gates"), ACT.Tanh).then_inc(s["gates_done"], 1)
            stages(enter, body, act.Fori)

        @block.vector
        def _(dve):
            def spread(src, name, done, settle):
                for qt in range(2):
                    done(dve.bn_stats(stats[name][:, qt], src[:, qt]))
                settle(apart=True)
                for qt in range(2):
                    last = dve.bn_aggr(mv[name][:, qt], stats[name][:, qt])
                last.then_inc(s[name + "_stats"], 1)

            def center(src, b, name, dst, dst_sem):
                dve.wait_ge(s[name + "_rstd"], b + 1)
                for qt in range(2):
                    last = dve.tensor_scalar(dst[:, qt], src[:, qt], mv[name][:, qt, 0:1], rstd[name][:, qt:qt + 1],
                                             ALU.subtract, ALU.mult)
                last.then_inc(dst_sem, 1)

            def batch_bias(b):
                if not first_of(b):
                    dve.wait_ge(s["exp_sb"][1], 8 * b)
                dve.tensor_copy(ebias[:], ebc[:, bass.ds(b, 1)].rearrange("p o k -> p (o k)")).then_inc(s["batch_bias"], 1)
                dve.tensor_copy(kbrow[:], kbr[:, bass.ds(b * S, S)].bitcast(F32)).then_inc(s["batch_bias"], 1)

            def keys_values(b, l):
                dve.wait_ge(s["k_hi"][l], b + 1)
                dve.scalar_tensor_tensor(kl[l][:], SC[:, 3, 0:S], c("bk")[:, l:l + 1], kh[l][:].bitcast(F32),
                                         ALU.add, ALU.subtract).then_inc(s["k_lo"][l], 1)
                dve.wait_ge(s["v_ps"][l], b + 1)
                if first_of(b):
                    dve.wait_ge(s["ones_set"], 4)
                for slot in range(2):
                    hs = slice(8 * slot, 8 * slot + 8)
                    dve.tensor_tensor(
                        vst[l][:, :, hs, 8 * slot:8 * slot + 8],
                        SC[:, 1, 0:S].rearrange("p (k h d) -> p k h d", k=2, d=HD)[:, :, hs],
                        c("bv")[:, 128 * l:128 * l + 128].rearrange("p (o h d) -> p o h d", o=1, d=HD)[:, :, hs].to_broadcast([128, 2, 8, HD]),
                        ALU.add).then_inc(s["v_sb"][l], 1)

            def queries(b, l):
                dve.wait_ge(s["q_hi"][l], b + 1)
                dve.scalar_tensor_tensor(ql[l][:], SC[:, 2, 0:S], c("bq")[:, l:l + 1], qh[l][:].bitcast(F32),
                                         ALU.add, ALU.subtract).then_inc(s["q_lo"][l], 1)

            def stacks(b, l):
                for half, bank in ((0, 2), (1, 1)):
                    dve.wait_ge(s["qstack_ps"][l], 2 * b + half + 1)
                    dve.tensor_scalar(qs[l][:, 2 * half:2 * half + 2].rearrange("p t q -> p (t q)"), SC[:, bank],
                                      c("qaux"), None, ALU.add).then_inc(s["qstack_sb"][l], 1)

            def max_unit(b, l, n):
                qt, tp, u = unit(n)
                dve.wait_ge(s["s_ps"][l], 8 * b + n + 1)
                scores = SC[:, 2 * u:2 * u + 2].rearrange("p i (t k) -> p i t k", t=2)
                if l == 1:
                    parts = [(0, 128, 0, 256)]
                elif qt == 0:
                    parts = [(0, 64, 0, 64), (64, 128, 64, 128)]
                else:
                    parts = [(0, 64, 0, 256), (64, 128, 192, 256)]
                for p0, p1, k0, k1 in parts:
                    last = dve.tensor_reduce(mx[l][p0:p1, qt, 2 * u:2 * u + 2, 2 * tp:2 * tp + 2],
                                             scores[p0:p1, :, :, k0:k1], AX, ALU.max)
                last.then_inc(s["s_max"][l], 1)

            def sums(src, done, settle):
                done(dve.stream_shuffle(sh[:], src[:], [16 + r % 16 for r in range(32)]))
                settle()
                done(dve.reciprocal(rsh[:], sh[:]))

            def normalize(l, src, settle):
                settle()
                dve.tensor_tensor(on[l][:].rearrange("p a q -> p (a q)"), src[:], rsh[:], ALU.mult).then_inc(s["on_sb"][l], 1)

            def router(m, done, settle):
                dve.wait_ge(s["logits_ps"], m + 1)
                done(dve.tensor_tensor(lg[:], PV[:, 0:2 * E].rearrange("p (q e) -> p q e", q=2),
                                       c("br").unsqueeze(1).to_broadcast([128, 2, E]), ALU.add))
                settle(apart=True)
                for qt in range(2):
                    done(dve.max(top[:, qt], lg[:, qt]))
                settle()
                dve.tensor_tensor(gap[:], top[:, :, 1:2], top[:, :, 0:1], ALU.subtract).then_inc(s["gap_sb"], 1)
                for qt in range(2):
                    done(dve.max_index(topi[:, qt], top[:, qt], lg[:, qt]))
                settle()
                done(dve.tensor_copy(topf[:], topi[:]))

            def router_weights(m, done, settle):
                dve.wait_ge(s["egap_sb"], m + 1)
                done(dve.tensor_scalar(den[:], egap[:], 1.0, None, ALU.add))
                settle()
                done(dve.reciprocal(tw[:, :, 0:1], den[:]))
                settle()
                done(dve.tensor_tensor(tw[:, :, 1:2], egap[:], tw[:, :, 0:1], ALU.mult))
                settle()
                for qt in range(2):
                    dve.tensor_scalar(r1[:, qt], c("iota"), topf[:, qt, 0:1], tw[:, qt, 0:1], ALU.is_equal, ALU.mult)
                    last = dve.tensor_scalar(r2[:, qt], c("iota"), topf[:, qt, 1:2], tw[:, qt, 1:2], ALU.is_equal, ALU.mult)
                done(last)
                settle()
                done(dve.tensor_tensor(rw[:], r1[:], r2[:], ALU.add))
                settle()
                done(dve.tensor_copy(wc[:, :, 0:E], rw[:]))
                settle()
                dve.tensor_tensor(wc[:, :, E:2 * E], rw[:], wc[:, :, 0:E].bitcast(F32), ALU.subtract).then_inc(s["weights_sb"], 1)

            def step(m, g):
                if g % 4 == 3 and g >= 7:
                    e = g // 4 - 1
                    if e % 2 == 0:
                        dve.wait_ge(s["wbc_sb"], 4 * m + e // 2 + 1)
                    dve.wait_ge(s["o_ps"], E * m + e + 1)
                    if e >= 2:
                        dve.wait_ge(s["acc_sb"], E * m + e - 1)
                    dve.scalar_tensor_tensor(te[:, e % 2], OP[:, 0:S], c("b2")[:, e:e + 1], wbc[:, e],
                                             ALU.add, ALU.mult).then_inc(s["te_sb"], 1)

            def moe_spread(m, done, settle):
                dve.wait_ge(s["zT_ps"], m + 1)
                for qt in range(2):
                    done(dve.bn_stats(zst[:, qt], OP[:, qt * 128:qt * 128 + 128]))
                settle(apart=True)
                for qt in range(2):
                    last = dve.bn_aggr(zmv[:, qt], zst[:, qt])
                last.then_inc(s["z_stats"], 1)

            def moe_center(m):
                dve.wait_ge(s["z_rstd"], m + 1)
                for qt in range(2):
                    last = dve.tensor_scalar(zn[:, qt], OP[:, qt * 128:qt * 128 + 128], zmv[:, qt, 0:1], zrs[:, qt:qt + 1],
                                             ALU.subtract, ALU.mult)
                last.then_inc(s["zn_sb"], 1)

            def enter(b):
                done, settle, _ = counted(dve, s["next_step"], NEXT_STEPS * b)
                dve.wait_ge(s["x_in"], 16 * b + 16)
                spread(xin, "lnx", done, settle)
                center(xin, b, "lnx", xn[0], s["xn_sb"][0])
                keys_values(b, 0)
                queries(b, 0)
                dve.wait_ge(s["sel_in"], 16)
                dve.tensor_copy(rnd[:], sel_raw).then_inc(s["rounded"], 1)
                stacks(b, 0)

            def body(b0, b1, m, nxt):
                def steps(gs):
                    for g in gs if m is not None else ():
                        step(m, g)

                none = (None,) * 3
                n_done, n_settle, n_n = counted(dve, s["next_step"], nxt * NEXT_STEPS) if nxt is not None else none
                a_done, a_settle, a_n = counted(dve, s["attn0_step"], b0 * ATTN0_STEPS) if b0 is not None else none
                y_done, y_settle, y_n = counted(dve, s["attn1_step"], b1 * ATTN1_STEPS) if b1 is not None else none
                z_done, z_settle, z_n = counted(dve, s["moe_step"], m * MOE_STEPS) if m is not None else none
                for n in range(8):
                    if b0 is not None:
                        max_unit(b0, 0, n)
                    if m is not None:
                        if n == 1:
                            router(m, z_done, z_settle)
                        if n == 2:
                            router_weights(m, z_done, z_settle)
                    steps(S0_STEPS[n])
                if b1 is not None:
                    batch_bias(b1)
                    keys_values(b1, 1)
                steps(MID_STEPS[0])
                if b1 is not None:
                    queries(b1, 1)
                steps(MID_STEPS[1])
                steps(MID_STEPS[2])
                if b1 is not None:
                    stacks(b1, 1)
                steps(MID_STEPS[3])
                for n in range(8):
                    if b1 is not None:
                        max_unit(b1, 1, n)
                    steps(S1_STEPS[n])
                if nxt is not None:
                    dve.wait_ge(s["x_in"], 16 * nxt + 16)
                    spread(xin, "lnx", n_done, n_settle)
                    center(xin, nxt, "lnx", xn[0], s["xn_sb"][0])
                for n in range(8):
                    steps(A0_STEPS[n])
                for n in range(8):
                    if n == 2 and b0 is not None:
                        wait_apart(dve, s["pvs_sb"], b0 + 1)
                        sums(pvs, a_done, a_settle)
                        normalize(0, pvs, a_settle)
                    if n == PROJECT_AT and b0 is not None:
                        dve.wait_ge(s["y_ps"][0], b0 + 1)
                        dve.scalar_tensor_tensor(x1[:], OP[:, S:2 * S].rearrange("p (q d) -> p q d", q=2), gate[:, 0:1],
                                                 xres[:], ALU.mult, ALU.add).then_inc(s["x1_sb"], 1)
                        dve.wait_ge(s["x1_sb"], b0 + 1)
                        spread(x1, "lnf", a_done, a_settle)
                        center(x1, b0, "lnf", xf, s["xf_sb"])
                        dve.wait_ge(s["xf_sb"], b0 + 1)
                        quantize(dve, a_done, a_settle, xf[:].rearrange("p q (n k) -> p (q n) k", k=32), 2 * NB, xd[:],
                                 s["xd_sb"])
                    steps(A1_STEPS[n])
                steps(TAIL_STEPS[0])
                if b1 is not None:
                    wait_apart(dve, s["pv_ps"][1], b1 + 1)
                    sums(PV, y_done, y_settle)
                    normalize(1, PV, y_settle)
                if nxt is not None:
                    keys_values(nxt, 0)
                steps(TAIL_STEPS[1])
                steps(TAIL_STEPS[2])
                if nxt is not None:
                    queries(nxt, 0)
                steps(TAIL_STEPS[3])
                steps(TAIL_STEPS[4])
                if b1 is not None:
                    dve.wait_ge(s["y_ps"][1], b1 + 1)
                    if not first_of(b1):
                        dve.wait_ge(s["xb3_sb"], b1)
                    dve.scalar_tensor_tensor(x3[:], PV[:, 0:S].rearrange("p (q d) -> p q d", q=2), gate[:, 2:3],
                                             x2[:], ALU.mult, ALU.add).then_inc(s["x3_sb"], 1)
                    dve.wait_ge(s["x3_sb"], b1 + 1)
                if b0 is not None:
                    dve.wait_ge(s["ffn_ps"], b0 + 1)
                    dve.wait_ge(s["x1b_sb"], b0 + 1)
                    dve.scalar_tensor_tensor(x2[:], SC[:, 0, 0:S].rearrange("p (q d) -> p q d", q=2), gate[:, 1:2],
                                             x1b[:], ALU.mult, ALU.add).then_inc(s["x2_sb"], 1)
                if b1 is not None:
                    spread(x3, "lnz", y_done, y_settle)
                steps(TAIL_STEPS[5])
                if b0 is not None:
                    dve.wait_ge(s["x2_sb"], b0 + 1)
                    spread(x2, "lny", a_done, a_settle)
                if b1 is not None:
                    if not first_of(b1):
                        dve.wait_ge(s["x3T_ps"], b1)
                    center(x3, b1, "lnz", x3n, s["x3n_sb"])
                if nxt is not None:
                    stacks(nxt, 0)
                if b0 is not None:
                    center(x2, b0, "lny", xn[1], s["xn_sb"][1])
                steps(TAIL_STEPS[6])
                if m is not None:
                    moe_spread(m, z_done, z_settle)
                    moe_center(m)
                for got, want in ((n_n, NEXT_STEPS), (a_n, ATTN0_STEPS), (y_n, ATTN1_STEPS), (z_n, MOE_STEPS)):
                    assert got is None or got[0] == want, (got, want)

            dve.sem_inc(s["zn_sb"], 1)
            dve.wait_ge(s["const_in"], 16)
            enter(0)
            p_done, p_settle, _ = counted(dve, s["prep_step"], 0)
            dve.wait_ge(s["side_in"], 64)
            for side, mask, kb, keep, pen in ((sidec, maskc, kbc, keepc, penc), (sider, maskr, kbb, keepr, penr)):
                p_done(dve.scalar_tensor_tensor(keep[:], side[:], 1.0 / SCALE, mask[:], ALU.mult, ALU.mult))
                p_done(dve.tensor_scalar(pen[:], mask[:], -1.0, FAR, ALU.add, ALU.mult))
                p_settle()
                p_done(dve.tensor_tensor(kb[:], keep[:], pen[:], ALU.add))
                p_settle()
            dve.sem_inc(s["bias_rows"], 1)
            p_done(dve.tensor_scalar(penc[:], maskc[:], -1.0, 3e38, ALU.add, ALU.mult))
            p_done(dve.scalar_tensor_tensor(keepc[:], kbc[:].bitcast(F32), -SCALE, sidec[:], ALU.mult, ALU.add))
            p_settle()
            p_done(dve.tensor_tensor(ebc[:], keepc[:], penc[:], ALU.add))
            p_settle()
            dve.wait_ge(s["ffn_w_in"], 16)
            quantize(dve, p_done, p_settle, wfr[:].rearrange("p (n k) -> p n k", k=32), NB,
                     wdq[:].rearrange("p (n k) -> p n k", k=32), s["wd_quant"])
            dve.wait_ge(s["gates_done"], 1)
            dve.wait_ge(s["wd_quant"], 1)
            dve.wait_ge(s["bias_row_in"], 16)
            stages(lambda b: None, body, dve.Fori)

        @block.gpsimd
        def _(pool):
            def root(name, k, mv_, ve, rs):
                wait_apart(pool, s[name + "_stats"], k)
                pool.tensor_scalar(ve[:].unsqueeze(2), mv_[:, :, 1:2], EPS, None, ALU.add).then_inc(s[name + "_veps"], 1)
                pool.wait_ge(s[name + "_veps"], k)
                pool.tensor_tensor(rs[:], ve[:], halfs[:], ALU.pow).then_inc(s[name + "_rstd"], 1)

            def ln(name, b):
                root(name, b + 1, mv[name], veps[name], rstd[name])

            def mask_unit(b, n):
                tp, kt, u = unit(n)
                wait_apart(pool, s["exp_sb"][0], 8 * b + n + 1)

                def keep(rows, q0, per_q, per_key, base):
                    blk = P[0:rows, kt, 2 * tp + u, :, q0:q0 + 64]
                    pool.affine_select(out=blk, in_=blk, pattern=[[0, 4], [per_q, 64]], compare_op=ALU.is_ge, fill=0.0,
                                       base=base, channel_multiplier=per_key).then_inc(s["p_masked"], 1)
                if kt == 0:
                    keep(128, 0, 0, -1, 63)
                    keep(128, 64, 0, 1, -64)
                else:
                    keep(128, 192, 0, 1, -64)
                    keep(64, 128, 1, -1, 0)

            def step(m, g):
                if g % 4 == 3 and g >= 7:
                    e = g // 4 - 1
                    pool.wait_ge(s["te_sb"], E * m + e + 1)
                    if e == 0:
                        pool.wait_ge(s["x3T_sb"], m + 1)
                    else:
                        pool.wait_ge(s["acc_sb"], E * m + e)
                    pool.tensor_tensor(acc[:], x3T[:] if e == 0 else acc[:], te[:, e % 2], ALU.add).then_inc(s["acc_sb"], 1)

            def body(b0, b1, m, nxt):
                def steps(gs):
                    for g in gs if m is not None else ():
                        step(m, g)

                if m is not None:
                    pool.wait_ge(s["x3_sb"], m + 1)
                    pool.wait_ge(s["out_sb"], m + 1)
                    pool.tensor_tensor(xb3[:], x3[:], gbet[:].unsqueeze(1).to_broadcast([128, 2, D]), ALU.add)\
                        .then_inc(s["xb3_sb"], 1)
                for gs in S0_STEPS + MID_STEPS + S1_STEPS:
                    steps(gs)
                if nxt is not None:
                    ln("lnx", nxt)
                for n in range(8):
                    if b0 is not None:
                        mask_unit(b0, n)
                    steps(A0_STEPS[n])
                for n in range(8):
                    if n == PROJECT_AT and b0 is not None:
                        pool.wait_ge(s["x1_sb"], b0 + 1)
                        ln("lnf", b0)
                        pool.tensor_tensor(x1b[:], x1[:], gfb[:].unsqueeze(1).to_broadcast([128, 2, D]), ALU.add)\
                            .then_inc(s["x1b_sb"], 1)
                    steps(A1_STEPS[n])
                for gs in TAIL_STEPS[0:5]:
                    steps(gs)
                if b1 is not None:
                    ln("lnz", b1)
                steps(TAIL_STEPS[5])
                if b0 is not None:
                    ln("lny", b0)
                steps(TAIL_STEPS[6])
                if m is not None:
                    root("z", m + 1, zmv, zve, zrs)
                    pool.wait_ge(s["zn_sb"], m + 2)
                    pool.tensor_tensor(zg[:], zn[:], ggam[:].unsqueeze(1).to_broadcast([128, 2, D]), ALU.mult)\
                        .then_inc(s["zg_sb"], 1)
                    pool.wait_ge(s["zg_sb"], m + 1)
                    pool.wait_ge(s["stored"], 16 * m + 16)
                    pool.tensor_tensor(outt[:], zg[:], xb3[:], ALU.add).then_inc(s["out_sb"], 1)

            pool.memset(halfs[:], -0.5).then_inc(s["pool_prep"], 1)
            for l in range(2):
                pool.memset(vst[l][:], 0.0).then_inc(s["pool_prep"], 1)
            pool.wait_ge(s["pool_prep"], 3)
            ln("lnx", 0)
            for l in range(2):
                pool.memset(vst[l][:, :, 0:8, 16:24], 1.0).then_inc(s["ones_set"], 1)
                pool.memset(vst[l][:, :, 8:16, 24:32], 1.0).then_inc(s["ones_set"], 1)
            pool.memset(outt[:], 0.0).then_inc(s["out_sb"], 1)
            pool.wait_ge(s["gates_done"], 1)
            for src, dst, g in (("ffn_b", gfb, 1), ("gamma", ggam, 3), ("beta", gbet, 3)):
                pool.tensor_scalar(dst[:], c(src), gate[:, g:g + 1], None, ALU.mult).then_inc(s["pool_prep"], 1)
            pool.wait_ge(s["pool_prep"], 6)
            stages(lambda b: None, body, pool.Fori)


ORDER = np.concatenate([np.arange(0, 128), np.arange(192, 256), np.arange(128, 192)])


def head_of(tile, j, slot_):
    i, t = 2 * slot_ + j // 2, 2 * tile + j % 2
    return 4 * i + t


def tokens(a):
    return np.ascontiguousarray(a[:, ORDER].reshape(B, 2, 128, D).transpose(2, 0, 1, 3))


def constants(v):
    cst, selectors = np.zeros((128, NCONST), np.float32), np.zeros((128, NSEL), np.float32)

    def put(name, a):
        dst, (lo, hi) = (cst, CONST_AT[name]) if name in CONST_AT else (selectors, SEL_AT[name])
        a = np.asarray(a, np.float32)
        dst[0:a.shape[0], lo:hi] = a.reshape(a.shape[0], hi - lo)
    put("ident", np.eye(128))
    put("eye", np.eye(128))
    sel = np.zeros((128, 4, 4, 128), np.float32)
    for t in range(4):
        for i in range(4):
            for d in range(HD):
                ch, row = HD * (4 * i + t) + d, 32 * i + d
                for kind, rows in ((0, (0, 16)), (1, (8,)), (2, (0, 8)), (3, (16,))):
                    for r in rows:
                        sel[ch, kind, t, row + r] = 1
    put("sel", sel)
    aux = np.zeros((1, 128))
    aux[0, ROW_BIAS::32] = 1
    put("auxsel", aux)
    causal = np.zeros((128, 64))
    causal[0:64] = np.where(np.arange(64)[None] > np.arange(64)[:, None], -FAR, 0)
    put("causal", causal)
    wsel = np.zeros((2 * E, E, 128))
    for e in range(E):
        wsel[e, e] = wsel[E + e, e] = 1
    put("wsel", wsel)
    qaux, kaux = np.zeros((128, 1)), np.zeros((128, 1))
    qaux[ROW_BIAS::32] = 1
    kaux[ROW_MAX::32] = 1
    put("qaux", qaux)
    put("kaux", kaux)
    put("iota", np.tile(np.arange(E), (128, 1)))
    put("b1", v["L1_ffn_b1"].reshape(E * FB, 128).T)
    put("b2", v["L1_ffn_b2"].T)
    put("bq", np.stack([v["L0_xattn_bq"], v["L1_xattn_Wq_b"]], 1))
    put("bk", np.stack([v["L0_xattn_bk"], v["L1_xattn_Wkv_b"][0:D]], 1))
    g = [v["g_xattn"][0], v["g_ffn"][0], v["g_xattn"][1], v["g_ffn"][1]]
    for name, row in (("gates", g), ("bv", np.concatenate([v["L0_xattn_bv"], v["L1_xattn_Wkv_b"][D:]])),
                      ("ffn_b", v["L0_ffn_bias"]), ("gamma", v["L1_ffn_gamma"]), ("beta", v["L1_ffn_beta"]),
                      ("br", v["L1_ffn_br"])):
        put(name, np.broadcast_to(np.asarray(row)[None], (128, len(row))))
    return cst, selectors


def out_weight(w, b):
    o = np.zeros((128, 2, D), np.float32)
    for tile in range(2):
        for j in range(4):
            for slot_ in range(2):
                h, r = head_of(tile, j, slot_), 32 * j + 8 * slot_
                o[r:r + HD, tile] = w[HD * h:HD * h + HD]
    o[16, 0] = b
    return o


def kernel(**inputs):
    import concourse.bacc as bacc
    from concourse.bass_utils import run_bass_kernel_spmd

    v = {k: np.asarray(a) for k, a in inputs.items()}
    side, mask = v["fside_BxS2_0"][:, ORDER], v["mask_BxS2_bk0"][:, ORDER]
    wkv = v["L1_xattn_Wkv_w"]
    w_attn = np.zeros((128, 2, 5, D), np.float32)
    w_attn[:, 0, 0], w_attn[:, 0, 1], w_attn[:, 0, 2] = v["L0_xattn_Wq"], v["L0_xattn_Wk"], v["L0_xattn_Wv"]
    w_attn[:, 1, 0], w_attn[:, 1, 1], w_attn[:, 1, 2] = v["L1_xattn_Wq_w"].T, wkv[0:D].T, wkv[D:].T
    w_attn[:, 0, 3:] = out_weight(v["L0_xattn_Wo"], v["L0_xattn_bo"])
    w_attn[:, 1, 3:] = out_weight(v["L1_xattn_out_w"].T, v["L1_xattn_out_b"])
    cst, selectors = constants(v)
    arrays = {
        "x": tokens(v["x"]), "ctx": tokens(v["ctx_1024"]),
        "side_col": side.reshape(B, 2, 128).transpose(2, 0, 1), "mask_col": mask.reshape(B, 2, 128).transpose(2, 0, 1),
        "side_row": side, "mask_row": mask, "const": cst, "selectors": selectors,
        "w_attn": w_attn, "w_ffn": v["L0_ffn_weight"], "w_router": v["L1_ffn_Wr"].T,
        "w1": v["L1_ffn_W1"].reshape(E * FB, 128, D).transpose(2, 0, 1),
        "w2": v["L1_ffn_W2"].reshape(E, D, FB, 128).transpose(3, 0, 2, 1).reshape(128, E * FB, D),
    }
    arrays = {f"in_{k}": np.ascontiguousarray(a) for k, a in arrays.items()}
    nc = bacc.Bacc("TRN2", target_bir_lowering=False, num_devices=1)
    args = [nc.dram_tensor(k, a.shape, mybir.dt.from_np(a.dtype), kind="ExternalInput").ap() for k, a in arrays.items()]
    args.append(nc.dram_tensor("out_0", (128, B, 2, D), F32, kind="ExternalOutput").ap())
    program(nc, *args)
    got = run_bass_kernel_spmd(nc, [arrays], core_ids=[0]).results[0]["out_0"]
    back = np.argsort(ORDER)
    return np.ascontiguousarray(got.transpose(1, 2, 0, 3).reshape(B, S, D)[:, back])
```

```python
import numpy as np
import concourse.bass as bass
from concourse import mybir
from contextlib import ExitStack

F32 = mybir.dt.float32
F32R = mybir.dt.float32r
I32 = mybir.dt.int32
U32 = mybir.dt.uint32
U8 = mybir.dt.uint8
ALU = mybir.AluOpType
ACT = mybir.ActivationFunctionType
AX = mybir.AxisListType.X

B, S, D, H, E, F = 8, 256, 128, 16, 8, 512
HD = D // H
NB = D // 32
FB = F // 128
SCALE = HD ** -0.5
FAR = 1e30
EPS = 1e-5
ROW_MAX, ROW_BIAS = 24, 25

def columns(widths):
    at, n = {}, 0
    for name, w in widths:
        at[name] = (n, n + w)
        n += w
    return at, n


CONST_AT, NCONST = columns([("ident", 128), ("qaux", 1), ("kaux", 1), ("iota", E), ("b1", E * FB), ("b2", E), ("bq", 2),
                            ("bk", 2), ("gates", 4), ("bv", 2 * 128), ("ffn_b", 128), ("gamma", 128), ("beta", 128),
                            ("br", E)])
SEL_AT, NSEL = columns([("sel", 4 * 4 * 128), ("auxsel", 128), ("eye", 128), ("causal", 64), ("wsel", E * 128)])


def program(nc, x, ctx_in, side_col, mask_col, side_row, mask_row, const, selectors, w_attn, w_ffn, w_router, w1, w2, out):
    stack = ExitStack()
    with stack:
        def sb(name, shape, dt=F32):
            return stack.enter_context(nc.sbuf_tensor(name, shape, dt))

        def sem(name):
            return stack.enter_context(nc.semaphore(name))

        cst = sb("cst", [128, NCONST])
        rnd = sb("rnd", [128, NSEL], F32R)

        def c(name):
            a, b = CONST_AT[name]
            return cst[:, a:b]

        def cr(name):
            a, b = SEL_AT[name]
            return rnd[:, a:b]

        ident = c("ident")
        sel = cr("sel").rearrange("p (k t m) -> p k t m", k=4, t=4)
        wsel = cr("wsel").rearrange("p (e m) -> p e m", e=E)
        wat = sb("wat", [128, 2, 5, 128])
        wfr = sb("wfr", [128, 128])
        wdq = sb("wdq", [128, 128])
        wdT = sb("wdT", [128, 128])
        wrT = sb("wrT", [128, E])
        w1h = sb("w1h", [128, E * FB, 128], F32R)
        w1l = sb("w1l", [128, E * FB, 128], F32R)
        w2s = sb("w2s", [128, E * FB, 128])
        gate = sb("gate", [128, 4])
        gfb = sb("gfb", [128, 128])
        ggam = sb("ggam", [128, 128])
        gbet = sb("gbet", [128, 128])
        halfs = sb("halfs", [128, 2])
        sidec = sb("sidec", [128, B, 2])
        maskc = sb("maskc", [128, B, 2], U8)
        keepc = sb("keepc", [128, B, 2])
        penc = sb("penc", [128, B, 2])
        kbc = sb("kbc", [128, B, 2], F32R)
        ebc = sb("ebc", [128, B, 2])
        ebias = sb("ebias", [128, 2])
        maskr = sb("maskr", [B, S], U8)
        kbb = sb("kbb", [B, S], F32R)
        kbr = sb("kbr", [1, B * S], F32R)
        kbrow = sb("kbrow", [1, S], F32R)

        xin = sb("xin", [128, 2, D])
        xres = sb("xres", [128, 2, D])
        cin = sb("cin", [128, 2, D])
        x1 = sb("x1", [128, 2, D])
        x1b = sb("x1b", [128, 2, D])
        x2 = sb("x2", [128, 2, D])
        x3 = sb("x3", [128, 2, D])
        x3n = sb("x3n", [128, 2, D])
        stats, mv, veps, rstd = ({n: sb(f"{what}_{n}", shape) for n in ("lnx", "lnf", "lny", "lnz")} for what, shape in
                                 (("stats", [128, 2, 6]), ("mv", [128, 2, 2]), ("veps", [128, 2]), ("rstd", [128, 2])))
        def two(name, shape, dt=F32):
            return [sb(f"{name}{l}", shape, dt) for l in range(2)]
        xn = two("xn", [128, 2, D])
        ctxT = two("ctxT", [128, S])
        xnT = sb("xnT", [128, S])
        qh = sb("qh", [128, S], F32R)
        ql = sb("ql", [128, S], F32R)
        kh = sb("kh", [128, S], F32R)
        kl = sb("kl", [128, S], F32R)
        qs = two("qs", [128, 4, S], F32R)
        ks = two("ks", [128, 4, S], F32R)
        vst = two("vst", [128, 2, H, 32])
        mx = two("mx", [128, 2, 4, 4])
        mneg = two("mneg", [H, S], F32R)
        P = sb("P", [128, 2, 4, 4, S])
        pvs = sb("pvs", [128, 2 * S])
        sh = sb("sh", [128, 2 * S])
        rsh = sb("rsh", [128, 2 * S])
        sider, penr, keepr = sh[0:B, 0:S], sh[0:B, S:2 * S], rsh[0:B, 0:S]
        sel_raw = P[:].rearrange("p a b c q -> p (a b c q)")[:, 0:NSEL]
        on = two("on", [128, 2, S])
        xf = sb("xf", [128, 2, D])
        bmax = sb("bmax", [128, 2 * NB])
        scl = sb("scl", [128, 2 * NB])
        rscl = sb("rscl", [128, 2 * NB])
        yq = sb("yq", [128, 2 * NB, 32])
        eb = sb("eb", [128, 2 * NB, 32], I32)
        ib = sb("ib", [128, 2 * NB, 32], I32)
        rq = sb("rq", [128, 2 * NB, 32])
        ps_ = sb("ps_", [128, 2 * NB, 32])
        xd = sb("xd", [128, 2 * NB, 32])
        xdT = sb("xdT", [128, S])
        x3T = sb("x3T", [128, S])
        x3h = sb("x3h", [128, S], F32R)
        x3l = sb("x3l", [128, S], F32R)
        xb3 = sb("xb3", [128, 2, D])
        lg = sb("lg", [128, 2, E])
        top = sb("top", [128, 2, 8])
        topi = sb("topi", [128, 2, 8], U32)
        topf = sb("topf", [128, 2, 8])
        gap = sb("gap", [128, 2, 1])
        egap = sb("egap", [128, 2, 1])
        den = sb("den", [128, 2, 1])
        tw = sb("tw", [128, 2, 2])
        r1 = sb("r1", [128, 2, E])
        r2 = sb("r2", [128, 2, E])
        rw = sb("rw", [128, 2, E])
        wc = sb("wc", [128, 2, 2 * E], F32R)
        wT = sb("wT", [2 * E, S], F32R)
        wbc = sb("wbc", [128, E, S])
        hbuf = sb("hbuf", [128, 2, FB, S])
        w1_raw = [t.rearrange("p n m -> p (n m)") for t in
                  (wbc[:], hbuf[:].rearrange("p b f q -> p (b f) q"))]
        te = sb("te", [128, 2, S])
        acc = sb("acc", [128, S])
        zst = sb("zst", [128, 2, 6])
        zmv = sb("zmv", [128, 2, 2])
        zve = sb("zve", [128, 2])
        zrs = sb("zrs", [128, 2])
        zn = sb("zn", [128, 2, D])
        zg = sb("zg", [128, 2, D])
        outt = sb("outt", [128, 2, D])

        SC = stack.enter_context(nc.psum_tensor("SC", [128, 4, 512], F32))
        PV = stack.enter_context(nc.psum_tensor("PV", [128, 512], F32))
        HP = stack.enter_context(nc.psum_tensor("HP", [128, 2, 512], F32))
        OP = stack.enter_context(nc.psum_tensor("OP", [128, 512], F32))

        names = """apart const_in sel_in bias_rows bias_row_in attn0_w_in attn1_w_in ffn_w_in router_w_in w1_in w1_split
            w2_in side_in x_in ctx_in_ xres_sb rounded ones_set
            gates_done prep_step pool_prep wd_quant wdT_ps wdT_sb batch_bias
            lnx_stats lnx_veps lnx_rstd lnf_stats lnf_veps lnf_rstd lny_stats lny_veps lny_rstd lnz_stats lnz_veps lnz_rstd
            xf_sb x3n_sb ctxT_ps ctx0_sb ctx1_sb p_masked pvs_sb x1_sb x2_sb x3_sb x1b_sb xd_sb xdT_ps xdT_sb ffn_ps
            next_step attn0_step attn1_step x3T_ps x3T_sb x3h_sb x3l_sb xb3_sb logits_ps gap_sb egap_sb weights_sb
            wT_ps wT_sb wbc_ps wbc_sb
            h_ps relu_sb o_ps te_sb acc_sb zT_ps z_stats z_veps z_rstd zn_sb zg_sb out_sb stored moe_step""".split()
        s = {n: sem(n) for n in names}
        for n in """xn_sb k_ps v_ps xnT_ps xnT_sb q_ps k_hi q_hi k_lo q_lo v_sb kstack_ps qstack_ps kstack_sb qstack_sb
                s_ps s_max mxT_ps mneg_sb max_row st_ps exp_sb pv_ps on_sb y_ps""".split():
            s[n] = [sem(f"{n}{l}") for l in range(2)]

        NEXT_STEPS, ATTN0_STEPS, ATTN1_STEPS, MOE_STEPS = 2, 18, 4, 14

        S0_STEPS = ((), (), (0, 2), (4, 5), (6,), (7,), (8,), (9,))
        MID_STEPS = ((10,), (11,), (12,), (13,), (14, 15))
        X_STEPS = ((16,), (17,), (18,), (19,), (20,), (21,), (22,), (), (23,))
        A1_STEPS = ((24,), (26,), (), (), (), (), (25,), (27,))
        TAIL_STEPS = ((28,), (), (30,), (), (29,), (), (31,), (), (33, 35))
        PROJECT_AT, PROJECT_STEP = 3, 23

        def pair_of(n, other):
            return n % 2 if other is None else 0

        def first_of(b):
            return isinstance(b, int) and b == 0

        def counted(eng, semaphore, base):
            n = [0]

            def done(ins):
                n[0] += 1
                return ins.then_inc(semaphore, 1)

            def settle(apart=False):
                (wait_apart(eng, semaphore, base + n[0]) if apart else eng.wait_ge(semaphore, base + n[0]))
            return done, settle, n

        def wait_apart(eng, semaphore, value):
            eng.wait_ge(semaphore, value)
            if not isinstance(value, int):
                eng.sem_inc(s["apart"])

        def per_block(t, nb):
            return t[:, 0:nb].unsqueeze(2).to_broadcast([128, nb, 32])

        def fp6_scale(dve, done, settle, src, nb):
            v = slice(0, nb)
            done(dve.tensor_reduce(bmax[:, v], src, AX, ALU.max, apply_absolute_value=True))
            settle()
            done(dve.tensor_scalar(scl[:, v], bmax[:, v], 1.0 / 7.5, 1e-30, ALU.mult, ALU.max))
            settle()
            done(dve.reciprocal(rscl[:, v], scl[:, v]))
            settle()
            done(dve.tensor_tensor(yq[:, v], src, per_block(rscl, nb), ALU.mult))

        def fp6_round(dve, done, settle, nb, dst, last):
            v = slice(0, nb)
            settle()
            done(dve.tensor_scalar(eb[:, v], yq[:, v].bitcast(I32), 0x7F800000, None, ALU.bitwise_and))
            settle()
            done(dve.tensor_scalar(eb[:, v].bitcast(F32), eb[:, v].bitcast(F32), 1.0, 4.0, ALU.max, ALU.min))
            settle()
            done(dve.tensor_scalar(ib[:, v], eb[:, v], -1.0, float(257 << 23), ALU.mult, ALU.add))
            done(dve.tensor_tensor(ps_[:, v], eb[:, v].bitcast(F32), per_block(scl, nb), ALU.mult))
            settle()
            done(dve.tensor_tensor(yq[:, v], yq[:, v], ib[:, v].bitcast(F32), ALU.mult))
            settle()
            done(dve.tensor_scalar(rq[:, v], yq[:, v], 12582912.0, -12582912.0, ALU.add, ALU.add))
            settle()
            done(dve.tensor_tensor(yq[:, v], rq[:, v], yq[:, v], ALU.subtract))
            settle()
            done(dve.scalar_tensor_tensor(yq[:, v], yq[:, v], 0.5, rq[:, v], ALU.is_ge, ALU.subtract))
            settle()
            dve.scalar_tensor_tensor(dst, yq[:, v], -0.125, ps_[:, v], ALU.mult, ALU.mult).then_inc(last, 1)

        def q_range(l, kt):
            return (0, S) if l == 1 else ((0, 192), (128, 256))[kt]

        def unit(n):
            return n // 4, (n // 2) % 2, n % 2

        def flat(t):
            return t[:].rearrange("p q d -> p (q d)")

        def stages(enter, body, loop):
            enter(0)
            body(0, None, None, 1)
            body(1, 0, None, 2)
            with loop(0, B - 3) as m:
                body(m + 2, m + 1, m, m + 3)
            body(B - 1, B - 2, B - 3, None)
            body(None, B - 1, B - 2, None)
            body(None, None, B - 1, None)

        block = stack.enter_context(nc.Block())

        @block.sync
        def _(sp):
            def load(b):
                sp.dma_start(xin[:], x[:, bass.ds(b, 1)].rearrange("p o q d -> p (o q) d")).then_inc(s["x_in"], 16)
                sp.dma_start(cin[:], ctx_in[:, bass.ds(b, 1)].rearrange("p o q d -> p (o q) d")).then_inc(s["ctx_in_"], 16)

            def max_rows(b, l):
                sp.wait_ge(s["mneg_sb"][l], b + 1)
                sp.dma_start(qs[l][ROW_MAX:128:32, :, :].bitcast(F32),
                             mneg[l][:].bitcast(F32)).then_inc(s["max_row"][l], 16)

            def store(m):
                wait_apart(sp, s["out_sb"], m + 2)
                sp.dma_start(out[:, bass.ds(m, 1)].rearrange("p o q d -> p (o q) d"), outt[:]).then_inc(s["stored"], 16)

            def body(b0, b1, m, nxt):
                if nxt is not None:
                    sp.wait_ge(s["ctxT_ps"], b0 + 1)
                    sp.wait_ge(s["xn_sb"][0], b0 + 1)
                    wait_apart(sp, s["xres_sb"], b0 + 1)
                    load(nxt)
                if b0 is not None:
                    max_rows(b0, 0)
                if first_of(b0):
                    sp.wait_ge(s["bias_rows"], 1)
                    sp.dma_start(kbr[:].bitcast(F32), kbb[:].bitcast(F32)).then_inc(s["bias_row_in"], 16)
                if b1 is not None:
                    max_rows(b1, 1)
                if m is not None:
                    store(m)

            sp.sem_inc(s["stored"], 16)
            sp.dma_start(cst[:], const).then_inc(s["const_in"], 16)
            sp.dma_start(wat[:, 0], w_attn[:, 0]).then_inc(s["attn0_w_in"], 16)
            load(0)
            sp.dma_start(sel_raw, selectors).then_inc(s["sel_in"], 16)
            sp.dma_start(wfr[:], w_ffn).then_inc(s["ffn_w_in"], 16)
            for dst, src in ((sidec, side_col), (maskc, mask_col), (sider, side_row), (maskr, mask_row)):
                sp.dma_start(dst[:], src).then_inc(s["side_in"], 16)
            sp.dma_start(wat[:, 1], w_attn[:, 1]).then_inc(s["attn1_w_in"], 16)
            sp.dma_start(wrT[:], w_router).then_inc(s["router_w_in"], 16)
            for half in range(2):
                n = E * FB // 2
                sp.dma_start(w1_raw[half].rearrange("p (n m) -> p n m", m=128),
                             w1[:, n * half:n * half + n]).then_inc(s["w1_in"], 16)
            sp.dma_start(w2s[:], w2).then_inc(s["w2_in"], 16)
            stages(lambda b: None, body, sp.Fori)
            sp.wait_ge(s["stored"], 16 * B + 16)

        @block.tensor
        def _(pe):
            def transpose2(dst, src):
                for t in range(2):
                    last = pe.transpose(dst[:, t * 128:(t + 1) * 128], src[:, t * 128:(t + 1) * 128], ident)
                return last

            def keys_values(b, l):
                pe.matmul(SC[:, 3, 0:S], wat[:, l, 1], ctxT[l][:], start=True, stop=True).then_inc(s["k_ps"][l], 1)
                for t in range(2):
                    last = pe.matmul(SC[:, 1, t * 128:(t + 1) * 128], ctxT[l][:, t * 128:(t + 1) * 128], wat[:, l, 2],
                                     start=True, stop=True)
                last.then_inc(s["v_ps"][l], 1)

            def turn_ctx(b):
                pe.wait_ge(s["ctx_in_"], 16 * b + 16)
                transpose2(SC[:, 1], flat(cin)).then_inc(s["ctxT_ps"], 1)

            def turn_x(b, l):
                pe.wait_ge(s["xn_sb"][l], b + 1)
                transpose2(SC[:, 0], flat(xn[l])).then_inc(s["xnT_ps"][l], 1)

            def queries(b, l):
                pe.wait_ge(s["xnT_sb"][l], b + 1)
                pe.matmul(SC[:, 2, 0:S], wat[:, l, 0], xnT[:], start=True, stop=True).then_inc(s["q_ps"][l], 1)

            def stack_keys(b, l):
                if first_of(b) and l == 0:
                    pe.wait_ge(s["rounded"], 2)
                pe.wait_ge(s["k_lo"][l], b + 1)
                if l == 1:
                    pe.wait_ge(s["batch_bias"], 2 * b + 2)
                for half, bank in ((0, 3), (1, 0)):
                    for tt in range(2):
                        o = SC[:, bank, tt * S:(tt + 1) * S]
                        t = 2 * half + tt
                        pe.matmul(o, sel[:, 2, t], kh[:], start=True, stop=False)
                        last = pe.matmul(o, sel[:, 3, t], kl[:], start=False, stop=l == 0)
                        if l == 1:
                            last = pe.matmul(o, cr("auxsel")[0:1, :], kbrow[:], start=False, stop=True)
                    last.then_inc(s["kstack_ps"][l], 1)

            def stack_queries(b, l):
                pe.wait_ge(s["q_lo"][l], b + 1)
                pe.wait_ge(s["v_sb"][l], 2 * b + 2)
                for half, bank in ((0, 2), (1, 1)):
                    for tt in range(2):
                        o = SC[:, bank, tt * S:(tt + 1) * S]
                        t = 2 * half + tt
                        pe.matmul(o, sel[:, 0, t], qh[:], start=True, stop=False)
                        last = pe.matmul(o, sel[:, 1, t], ql[:], start=False, stop=True)
                    last.then_inc(s["qstack_ps"][l], 1)

            def score_unit(b, l, n, pair, single=False):
                if n == 0:
                    pe.wait_ge(s["kstack_sb"][l], 2 * b + 2)
                    pe.wait_ge(s["qstack_sb"][l], 2 * b + 2)
                qt, tp, u = unit(n)
                if single and n >= 1:
                    pe.wait_ge(s["s_max"][l], 8 * b + n)
                elif n >= 2:
                    pe.wait_ge(s["s_max"][l], 8 * b + n - 1)
                nk = 128 if l == 0 and qt == 0 else S
                masked = l == 0 and qt == 1
                for tt in range(2):
                    for i in (2 * u, 2 * u + 1):
                        r = slice(32 * i, 32 * i + 32)
                        last = pe.matmul(SC[:, 2 * pair + i % 2, tt * S:tt * S + nk], qs[l][r, 2 * tp + tt, qt * 128:qt * 128 + 128],
                                         ks[l][r, 2 * tp + tt, 0:nk], start=True, stop=not masked, skip_group_check=masked)
                if masked:
                    for i in (2 * pair, 2 * pair + 1):
                        last = pe.matmul(SC[:, i].rearrange("p (t k) -> p t k", t=2)[:, :, 128:192], cr("eye"),
                                         cr("causal").unsqueeze(1).to_broadcast([128, 2, 64]),
                                         start=False, stop=True, skip_group_check=True)
                last.then_inc(s["s_ps"][l], 1)

            def max_out(b, l):
                pe.wait_ge(s["s_max"][l], 8 * b + 8)
                dst = PV if l == 0 else SC[:, 0]
                for qt in range(2):
                    last = pe.transpose(dst[0:H, qt * 128:qt * 128 + 128], mx[l][:, qt].rearrange("p i t -> p (i t)"), ident)
                last.then_inc(s["mxT_ps"][l], 1)

            def attend_unit(b, l, n, pair, single=False):
                if n == 0:
                    pe.wait_ge(s["max_row"][l], 16 * b + 16)
                tp, kt, u = unit(n)
                if single and n >= 1:
                    pe.wait_ge(s["exp_sb"][l], 8 * b + n)
                elif n >= 2:
                    pe.wait_ge(s["exp_sb"][l], 8 * b + n - 1)
                a, z = q_range(l, kt)
                for tt in range(2):
                    for i in (2 * u, 2 * u + 1):
                        r = slice(32 * i, 32 * i + 32)
                        last = pe.matmul(SC[:, 2 * pair + i % 2, tt * S:tt * S + z - a], ks[l][r, 2 * tp + tt, kt * 128:kt * 128 + 128],
                                         qs[l][r, 2 * tp + tt, a:z], start=True, stop=True)
                last.then_inc(s["st_ps"][l], 1)

            def weigh(b, l, n):
                tp, kt, u = unit(n)
                if l == 0:
                    pe.wait_ge(s["p_masked"], 16 * b + 2 * n + 2)
                else:
                    pe.wait_ge(s["exp_sb"][1], 8 * b + n + 1)
                parts = [q_range(l, kt)] if l == 1 or kt == 0 else [(128, 192), (192, 256)]
                for tt in range(2):
                    for ii in range(2):
                        i, t, j = 2 * u + ii, 2 * tp + tt, 2 * ii + tt
                        for a, z in parts:
                            last = pe.matmul(PV[32 * j:32 * j + 32, tp * S + a:tp * S + z], vst[l][:, kt, 4 * i + t],
                                             P[:, kt, 2 * tp + u, 2 * ii + tt, a:z], start=(kt == 0 and u == 0),
                                             stop=(kt == 1 and u == 1), skip_group_check=True)
                if n == 7:
                    last.then_inc(s["pv_ps"][l], 1)

            def project(b, l, dst):
                pe.wait_ge(s["on_sb"][l], b + 1)
                for qt in range(2):
                    for ab in range(2):
                        last = pe.matmul(dst[:, qt * 128:qt * 128 + 128], on[l][:, ab, qt * 128:qt * 128 + 128],
                                         wat[:, l, 3 + ab], start=(ab == 0), stop=(ab == 1))
                last.then_inc(s["y_ps"][l], 1)

            def ffn_turn(b):
                pe.wait_ge(s["xd_sb"], b + 1)
                transpose2(SC[:, 0], xd[:].rearrange("p n k -> p (n k)")).then_inc(s["xdT_ps"], 1)

            def ffn_out(b):
                pe.wait_ge(s["xdT_sb"], b + 1)
                for qt in range(2):
                    last = pe.matmul(PV[:, S + qt * 128:S + qt * 128 + 128], xdT[:, qt * 128:qt * 128 + 128], wdT[:],
                                     start=True, stop=True)
                last.then_inc(s["ffn_ps"], 1)

            def moe_in(m):
                pe.wait_ge(s["x3n_sb"], m + 1)
                transpose2(HP[:, 0], flat(x3n)).then_inc(s["x3T_ps"], 1)

            def logits(m):
                pe.wait_ge(s["x3T_sb"], m + 1)
                for qt in range(2):
                    last = pe.matmul(PV[:, qt * E:qt * E + E], x3T[:, qt * 128:qt * 128 + 128], wrT[:],
                                     start=True, stop=True)
                last.then_inc(s["logits_ps"], 1)

            def moe_weights(m, g):
                if g == 0:
                    pe.wait_ge(s["weights_sb"], m + 1)
                    for qt in range(2):
                        last = pe.transpose(PV[0:2 * E, qt * 128:qt * 128 + 128], wc[:, qt].bitcast(F32), ident)
                    last.then_inc(s["wT_ps"], 1)
                    pe.wait_ge(s["wT_sb"], m + 1)
                else:
                    pe.wait_ge(s["wbc_sb"], 4 * m + g)
                for e in (2 * g, 2 * g + 1):
                    last = pe.matmul(PV[:, (e % 2) * S:(e % 2) * S + S], wsel[0:2 * E, e], wT[:], start=True, stop=True)
                last.then_inc(s["wbc_ps"], 1)

            def step(m, g, b0):
                e, p = g // 4, (g % 4) // 2
                if g % 2 == 0 and e < E:
                    if e >= 1:
                        pe.wait_ge(s["relu_sb"], 4 * E * m + 4 * (e - 1) + 2 * p + 2)
                    if e == 0 and p == 0:
                        pe.wait_ge(s["x3l_sb"], m + 1)
                    for k in range(2):
                        f, dst = FB * e + 2 * p + k, HP[:, p, k * S:(k + 1) * S]
                        pe.matmul(dst, w1h[:, f], x3h[:], start=True, stop=False)
                        pe.matmul(dst, w1h[:, f], x3l[:], start=False, stop=False)
                        last = pe.matmul(dst, w1l[:, f], x3h[:], start=False, stop=True)
                    last.then_inc(s["h_ps"], 1)
                if g % 2 == 1 and e >= 1:
                    if p == 0 and e >= 2:
                        pe.wait_ge(s["te_sb"], E * m + e - 1)
                    if e == 1 and p == 0:
                        pe.wait_ge(s["zn_sb"], m + 1)
                    if g == PROJECT_STEP + 2 and b0 is not None:
                        pe.wait_ge(s["x1_sb"], b0 + 1)
                    pe.wait_ge(s["relu_sb"], 4 * E * m + 4 * (e - 1) + 2 * p + 2)
                    for k in (2 * p, 2 * p + 1):
                        last = pe.matmul(OP[:, 0:S], w2s[:, FB * (e - 1) + k], hbuf[:, (e - 1) % 2, k],
                                         start=(k == 0), stop=(k == FB - 1))
                    if p == 1:
                        last.then_inc(s["o_ps"], 1)

            def moe_out(m):
                pe.wait_ge(s["acc_sb"], E * m + E)
                transpose2(OP, acc[:]).then_inc(s["zT_ps"], 1)

            def enter(b):
                turn_ctx(b)
                pe.wait_ge(s["ctx0_sb"], b + 1)
                keys_values(b, 0)
                turn_x(b, 0)
                queries(b, 0)
                stack_keys(b, 0)
                stack_queries(b, 0)
                for n in range(2):
                    score_unit(b, 0, n, n % 2)

            def body(b0, b1, m, nxt):
                def steps(gs):
                    for g in gs if m is not None else ():
                        step(m, g, b0)

                for n in range(8):
                    if b0 is not None and n >= 2:
                        score_unit(b0, 0, n, n % 2)
                    if m is not None:
                        if n == 2:
                            logits(m)
                        if n >= 4:
                            moe_weights(m, n - 4)
                    steps(S0_STEPS[n])
                if b0 is not None:
                    if m is not None:
                        pe.wait_ge(s["wbc_sb"], 4 * m + 4)
                    max_out(b0, 0)
                if b1 is not None:
                    pe.wait_ge(s["ctx1_sb"], b1 + 1)
                    keys_values(b1, 1)
                    turn_x(b1, 1)
                steps(MID_STEPS[0])
                if b1 is not None:
                    queries(b1, 1)
                steps(MID_STEPS[1])
                if b1 is not None:
                    stack_keys(b1, 1)
                steps(MID_STEPS[2])
                if b1 is not None:
                    stack_queries(b1, 1)
                steps(MID_STEPS[3])
                if b1 is not None:
                    score_unit(b1, 1, 0, 0)
                steps(MID_STEPS[4])
                if b1 is not None:
                    score_unit(b1, 1, 1, pair_of(1, b0), single=b0 is not None)
                for n in range(8):
                    if b0 is not None:
                        attend_unit(b0, 0, n, 1 - pair_of(n, b1), single=b1 is not None)
                    if b1 is not None and n == 6:
                        max_out(b1, 1)
                    steps(X_STEPS[n])
                    if b1 is not None and n < 6:
                        score_unit(b1, 1, n + 2, pair_of(n, b0), single=b0 is not None)
                    if b0 is not None and n >= 1:
                        if n == 1:
                            pe.wait_ge(s["mneg_sb"][0], b0 + 1)
                        weigh(b0, 0, n - 1)
                steps(X_STEPS[8])
                if b0 is not None:
                    weigh(b0, 0, 7)
                for n in range(8):
                    if b1 is not None:
                        if n == 1 and b0 is not None:
                            pe.wait_ge(s["exp_sb"][0], 8 * b0 + 8)
                        attend_unit(b1, 1, n, n % 2)
                    if b1 is not None and n >= 2:
                        if n == 2 and b0 is not None:
                            pe.wait_ge(s["pvs_sb"], b0 + 1)
                        weigh(b1, 1, n - 2)
                    if n == PROJECT_AT and b0 is not None:
                        if m is not None:
                            pe.wait_ge(s["te_sb"], E * m + (PROJECT_STEP + 1) // 4 - 1)
                        project(b0, 0, OP[:, S:2 * S])
                    steps(A1_STEPS[n])
                if b1 is not None:
                    weigh(b1, 1, 6)
                if nxt is not None:
                    turn_ctx(nxt)
                steps(TAIL_STEPS[0])
                if b1 is not None:
                    weigh(b1, 1, 7)
                steps(TAIL_STEPS[1])
                if first_of(b0):
                    pe.wait_ge(s["wd_quant"], 1)
                    pe.transpose(SC[:, 3, 0:128], wdq[:], ident).then_inc(s["wdT_ps"], 1)
                    pe.wait_ge(s["wdT_sb"], 1)
                if nxt is not None:
                    pe.wait_ge(s["ctx0_sb"], nxt + 1)
                    keys_values(nxt, 0)
                if nxt is not None:
                    turn_x(nxt, 0)
                steps(TAIL_STEPS[2])
                steps(TAIL_STEPS[3])
                if nxt is not None:
                    queries(nxt, 0)
                if b0 is not None:
                    ffn_turn(b0)
                steps(TAIL_STEPS[4])
                steps(TAIL_STEPS[5])
                if b1 is not None:
                    pe.wait_ge(s["on_sb"][1], b1 + 1)
                if b0 is not None:
                    ffn_out(b0)
                if b1 is not None:
                    project(b1, 1, PV[:, 0:S])
                steps(TAIL_STEPS[6])
                if nxt is not None:
                    stack_keys(nxt, 0)
                steps(TAIL_STEPS[7])
                if nxt is not None:
                    stack_queries(nxt, 0)
                steps(TAIL_STEPS[8])
                for n in range(2):
                    if nxt is not None:
                        score_unit(nxt, 0, n, n % 2)
                if b1 is not None:
                    moe_in(b1)
                if m is not None:
                    moe_out(m)
                if first_of(b0):
                    pe.wait_ge(s["attn1_w_in"], 16)
                    pe.wait_ge(s["router_w_in"], 16)
                    pe.wait_ge(s["w1_split"], 4)
                    pe.wait_ge(s["w2_in"], 16)

            pe.wait_ge(s["const_in"], 16)
            pe.wait_ge(s["attn0_w_in"], 16)
            stages(enter, body, pe.Fori)

        @block.scalar
        def _(act):
            def ctx_keep(b, b1):
                if b1 is not None:
                    act.wait_ge(s["v_ps"][1], b1 + 1)
                act.activation(ctxT[1][:], ctxT[0][:], ACT.Copy).then_inc(s["ctx1_sb"], 1)

            def ctx_turned(b):
                act.wait_ge(s["ctxT_ps"], b + 1)
                if not first_of(b):
                    act.wait_ge(s["ctx1_sb"], b)
                act.activation(ctxT[0][:], SC[:, 1, 0:S], ACT.Copy).then_inc(s["ctx0_sb"], 1)

            def keys(b, l):
                act.wait_ge(s["k_ps"][l], b + 1)
                act.activation(kh[:], SC[:, 3, 0:S], ACT.Identity, bias=c("bk")[:, l:l + 1]).then_inc(s["k_hi"][l], 1)

            def x_turned(b, l):
                act.wait_ge(s["xnT_ps"][l], b + 1)
                act.activation(xnT[:], SC[:, 0, 0:S], ACT.Copy).then_inc(s["xnT_sb"][l], 1)

            def queries(b, l):
                act.wait_ge(s["q_ps"][l], b + 1)
                act.activation(qh[:], SC[:, 2, 0:S], ACT.Identity, bias=c("bq")[:, l:l + 1]).then_inc(s["q_hi"][l], 1)

            def stacks(b, l):
                for half, bank in ((0, 3), (1, 0)):
                    act.wait_ge(s["kstack_ps"][l], 2 * b + half + 1)
                    act.activation(ks[l][:, 2 * half:2 * half + 2].rearrange("p t k -> p (t k)"), SC[:, bank],
                                   ACT.Identity, bias=c("kaux")).then_inc(s["kstack_sb"][l], 1)

                for half, bank in ((0, 2), (1, 1)) if l == 0 else ():
                    act.wait_ge(s["qstack_ps"][0], 2 * b + half + 1)
                    act.activation(qs[0][:, 2 * half:2 * half + 2].rearrange("p t q -> p (t q)"), SC[:, bank],
                                   ACT.Identity, bias=c("qaux")).then_inc(s["qstack_sb"][0], 1)

            def max_out(b, l):
                act.wait_ge(s["mxT_ps"][l], b + 1)
                act.activation(mneg[l][:], (PV if l == 0 else SC[:, 0])[0:H, 0:S], ACT.Copy, scale=-1.0).then_inc(s["mneg_sb"][l], 1)

            def exp_unit(b, l, n, pair):
                tp, kt, u = unit(n)
                a, z = q_range(l, kt)
                act.wait_ge(s["st_ps"][l], 8 * b + n + 1)
                scores = SC[:, 2 * pair:2 * pair + 2].rearrange("p i (t q) -> p i t q", t=2)[:, :, :, 0:z - a]
                more = {"bias": ebias[:, kt:kt + 1]} if l == 1 else {}
                act.activation(P[:, kt, 2 * tp + u, :, a:z].rearrange("p (i t) q -> p i t q", i=2), scores, ACT.Exp,
                               scale=SCALE, **more).then_inc(s["exp_sb"][l], 1)

            def step(m, g):
                e, p = g // 4, (g % 4) // 2
                if g % 2 == 0 and e < E:
                    act.wait_ge(s["h_ps"], 2 * E * m + 2 * e + p + 1)
                    if e >= 2 and p == 0:
                        act.wait_ge(s["o_ps"], E * m + e - 1)
                    for k in range(2):
                        f = 2 * p + k
                        act.activation(hbuf[:, e % 2, f], HP[:, p, k * S:(k + 1) * S], ACT.Relu,
                                       bias=c("b1")[:, FB * e + f:FB * e + f + 1]).then_inc(s["relu_sb"], 1)

            def enter(b):
                ctx_turned(b)
                keys(b, 0)
                x_turned(b, 0)
                queries(b, 0)
                act.wait_ge(s["sel_in"], 16)
                act.activation(rnd[:, 0:NSEL // 2], sel_raw[:, 0:NSEL // 2], ACT.Copy).then_inc(s["rounded"], 1)
                stacks(b, 0)

            def body(b0, b1, m, nxt):
                def steps(gs):
                    for g in gs if m is not None else ():
                        step(m, g)

                if b0 is not None:
                    if not first_of(b0):
                        act.wait_ge(s["x1_sb"], b0)
                    act.activation(flat(xres), flat(xin), ACT.Copy).then_inc(s["xres_sb"], 1)
                for n in range(8):
                    if m is not None:
                        if n == 2:
                            act.wait_ge(s["gap_sb"], m + 1)
                            act.activation(egap[:], gap[:], ACT.Exp).then_inc(s["egap_sb"], 1)
                        if n == 4:
                            act.wait_ge(s["wT_ps"], m + 1)
                            act.activation(wT[:], PV[0:2 * E, 0:S], ACT.Copy).then_inc(s["wT_sb"], 1)
                        if n >= 4:
                            g = n - 4
                            act.wait_ge(s["wbc_ps"], 4 * m + g + 1)
                            act.activation(wbc[:, 2 * g:2 * g + 2].rearrange("p e q -> p (e q)"), PV[:],
                                           ACT.Copy).then_inc(s["wbc_sb"], 1)
                    steps(S0_STEPS[n])
                if b0 is not None:
                    max_out(b0, 0)
                if b1 is not None:
                    keys(b1, 1)
                    x_turned(b1, 1)
                steps(MID_STEPS[0])
                if b1 is not None:
                    queries(b1, 1)
                steps(MID_STEPS[1])
                if b1 is not None:
                    stacks(b1, 1)
                for gs in MID_STEPS[2:]:
                    steps(gs)
                if b0 is not None:
                    ctx_keep(b0, b1)
                for n in range(8):
                    if b0 is not None:
                        exp_unit(b0, 0, n, 1 - pair_of(n, b1))
                    if b1 is not None and n == 6:
                        max_out(b1, 1)
                    steps(X_STEPS[n])
                steps(X_STEPS[8])
                if b0 is not None:
                    act.wait_ge(s["pv_ps"][0], b0 + 1)
                    act.activation(pvs[:], PV[:], ACT.Copy).then_inc(s["pvs_sb"], 1)
                for n in range(8):
                    if b1 is not None:
                        exp_unit(b1, 1, n, n % 2)
                    steps(A1_STEPS[n])
                if nxt is not None:
                    ctx_turned(nxt)
                steps(TAIL_STEPS[0])
                steps(TAIL_STEPS[1])
                if first_of(b0):
                    act.wait_ge(s["wdT_ps"], 1)
                    act.activation(wdT[:], SC[:, 3, 0:128], ACT.Copy).then_inc(s["wdT_sb"], 1)
                if nxt is not None:
                    keys(nxt, 0)
                if nxt is not None:
                    x_turned(nxt, 0)
                steps(TAIL_STEPS[2])
                steps(TAIL_STEPS[3])
                if nxt is not None:
                    queries(nxt, 0)
                if b0 is not None:
                    act.wait_ge(s["xdT_ps"], b0 + 1)
                    act.activation(xdT[:], SC[:, 0, 0:S], ACT.Copy).then_inc(s["xdT_sb"], 1)
                for gs in TAIL_STEPS[4:8]:
                    steps(gs)
                if nxt is not None:
                    stacks(nxt, 0)
                steps(TAIL_STEPS[8])
                if b1 is not None:
                    act.wait_ge(s["x3T_ps"], b1 + 1)
                    act.activation(x3T[:], HP[:, 0, 0:S], ACT.Copy).then_inc(s["x3T_sb"], 1)
                    act.activation(x3h[:], HP[:, 0, 0:S], ACT.Copy).then_inc(s["x3h_sb"], 1)

            act.wait_ge(s["const_in"], 16)
            act.activation(gate[:], c("gates"), ACT.Tanh).then_inc(s["gates_done"], 1)
            stages(enter, body, act.Fori)

        @block.vector
        def _(dve):
            def spread(src, name, done, settle):
                for qt in range(2):
                    done(dve.bn_stats(stats[name][:, qt], src[:, qt]))
                settle(apart=True)
                for qt in range(2):
                    last = dve.bn_aggr(mv[name][:, qt], stats[name][:, qt])
                last.then_inc(s[name + "_stats"], 1)

            def center(src, b, name, dst, dst_sem):
                dve.wait_ge(s[name + "_rstd"], b + 1)
                for qt in range(2):
                    last = dve.tensor_scalar(dst[:, qt], src[:, qt], mv[name][:, qt, 0:1], rstd[name][:, qt:qt + 1],
                                             ALU.subtract, ALU.mult)
                last.then_inc(dst_sem, 1)

            def batch_bias(b):
                if first_of(b):
                    dve.wait_ge(s["bias_row_in"], 16)
                else:
                    dve.wait_ge(s["exp_sb"][1], 8 * b)
                dve.tensor_copy(ebias[:], ebc[:, bass.ds(b, 1)].rearrange("p o k -> p (o k)")).then_inc(s["batch_bias"], 1)
                dve.tensor_copy(kbrow[:], kbr[:, bass.ds(b * S, S)].bitcast(F32)).then_inc(s["batch_bias"], 1)

            def keys_values(b, l):
                dve.wait_ge(s["k_hi"][l], b + 1)
                dve.scalar_tensor_tensor(kl[:], SC[:, 3, 0:S], c("bk")[:, l:l + 1], kh[:].bitcast(F32),
                                         ALU.add, ALU.subtract).then_inc(s["k_lo"][l], 1)
                dve.wait_ge(s["v_ps"][l], b + 1)
                if first_of(b):
                    dve.wait_ge(s["ones_set"], 4)
                for slot in range(2):
                    hs = slice(8 * slot, 8 * slot + 8)
                    dve.tensor_tensor(
                        vst[l][:, :, hs, 8 * slot:8 * slot + 8],
                        SC[:, 1, 0:S].rearrange("p (k h d) -> p k h d", k=2, d=HD)[:, :, hs],
                        c("bv")[:, 128 * l:128 * l + 128].rearrange("p (o h d) -> p o h d", o=1, d=HD)[:, :, hs].to_broadcast([128, 2, 8, HD]),
                        ALU.add).then_inc(s["v_sb"][l], 1)

            def queries(b, l):
                dve.wait_ge(s["q_hi"][l], b + 1)
                dve.scalar_tensor_tensor(ql[:], SC[:, 2, 0:S], c("bq")[:, l:l + 1], qh[:].bitcast(F32),
                                         ALU.add, ALU.subtract).then_inc(s["q_lo"][l], 1)

            def stacks(b, l):
                for half, bank in ((0, 2), (1, 1)):
                    dve.wait_ge(s["qstack_ps"][l], 2 * b + half + 1)
                    dve.tensor_scalar(qs[l][:, 2 * half:2 * half + 2].rearrange("p t q -> p (t q)"), SC[:, bank],
                                      c("qaux"), None, ALU.add).then_inc(s["qstack_sb"][l], 1)

            def max_unit(b, l, n, pair):
                qt, tp, u = unit(n)
                dve.wait_ge(s["s_ps"][l], 8 * b + n + 1)
                scores = SC[:, 2 * pair:2 * pair + 2].rearrange("p i (t k) -> p i t k", t=2)
                if l == 1:
                    parts = [(0, 128, 0, 256)]
                elif qt == 0:
                    parts = [(0, 64, 0, 64), (64, 128, 64, 128)]
                else:
                    parts = [(0, 64, 0, 256), (64, 128, 192, 256)]
                for p0, p1, k0, k1 in parts:
                    last = dve.tensor_reduce(mx[l][p0:p1, qt, 2 * u:2 * u + 2, 2 * tp:2 * tp + 2],
                                             scores[p0:p1, :, :, k0:k1], AX, ALU.max)
                last.then_inc(s["s_max"][l], 1)

            def sums(src, done, settle):
                done(dve.stream_shuffle(sh[:], src[:], [16 + r % 16 for r in range(32)]))
                settle()
                done(dve.reciprocal(rsh[:], sh[:]))

            def normalize(l, src, settle):
                settle()
                dve.tensor_tensor(on[l][:].rearrange("p a q -> p (a q)"), src[:], rsh[:], ALU.mult).then_inc(s["on_sb"][l], 1)

            def router(m, done, settle):
                dve.wait_ge(s["logits_ps"], m + 1)
                done(dve.tensor_tensor(lg[:], PV[:, 0:2 * E].rearrange("p (q e) -> p q e", q=2),
                                       c("br").unsqueeze(1).to_broadcast([128, 2, E]), ALU.add))
                settle(apart=True)
                for qt in range(2):
                    done(dve.max(top[:, qt], lg[:, qt]))
                settle()
                dve.tensor_tensor(gap[:], top[:, :, 1:2], top[:, :, 0:1], ALU.subtract).then_inc(s["gap_sb"], 1)
                for qt in range(2):
                    done(dve.max_index(topi[:, qt], top[:, qt], lg[:, qt]))
                settle()
                done(dve.tensor_copy(topf[:], topi[:]))

            def router_weights(m, done, settle):
                dve.wait_ge(s["egap_sb"], m + 1)
                done(dve.tensor_scalar(den[:], egap[:], 1.0, None, ALU.add))
                settle()
                done(dve.reciprocal(tw[:, :, 0:1], den[:]))
                settle()
                done(dve.tensor_tensor(tw[:, :, 1:2], egap[:], tw[:, :, 0:1], ALU.mult))
                settle()
                for qt in range(2):
                    dve.tensor_scalar(r1[:, qt], c("iota"), topf[:, qt, 0:1], tw[:, qt, 0:1], ALU.is_equal, ALU.mult)
                    last = dve.tensor_scalar(r2[:, qt], c("iota"), topf[:, qt, 1:2], tw[:, qt, 1:2], ALU.is_equal, ALU.mult)
                done(last)
                settle()
                done(dve.tensor_tensor(rw[:], r1[:], r2[:], ALU.add))
                settle()
                done(dve.tensor_copy(wc[:, :, 0:E], rw[:]))
                settle()
                dve.tensor_tensor(wc[:, :, E:2 * E], rw[:], wc[:, :, 0:E].bitcast(F32), ALU.subtract).then_inc(s["weights_sb"], 1)

            def step(m, g):
                if g % 4 == 3 and g >= 7:
                    e = g // 4 - 1
                    if e % 2 == 0:
                        dve.wait_ge(s["wbc_sb"], 4 * m + e // 2 + 1)
                    dve.wait_ge(s["o_ps"], E * m + e + 1)
                    if e >= 2:
                        dve.wait_ge(s["acc_sb"], E * m + e - 1)
                    dve.scalar_tensor_tensor(te[:, e % 2], OP[:, 0:S], c("b2")[:, e:e + 1], wbc[:, e],
                                             ALU.add, ALU.mult).then_inc(s["te_sb"], 1)

            def moe_spread(m, done, settle):
                dve.wait_ge(s["zT_ps"], m + 1)
                for qt in range(2):
                    done(dve.bn_stats(zst[:, qt], OP[:, qt * 128:qt * 128 + 128]))
                settle(apart=True)
                for qt in range(2):
                    last = dve.bn_aggr(zmv[:, qt], zst[:, qt])
                last.then_inc(s["z_stats"], 1)

            def moe_center(m):
                dve.wait_ge(s["z_rstd"], m + 1)
                for qt in range(2):
                    last = dve.tensor_scalar(zn[:, qt], OP[:, qt * 128:qt * 128 + 128], zmv[:, qt, 0:1], zrs[:, qt:qt + 1],
                                             ALU.subtract, ALU.mult)
                last.then_inc(s["zn_sb"], 1)

            def prepare():
                p_done, p_settle, _ = counted(dve, s["prep_step"], 0)
                dve.wait_ge(s["side_in"], 64)
                for side, mask, kb, keep, pen in ((sidec, maskc, kbc, keepc, penc), (sider, maskr, kbb, keepr, penr)):
                    p_done(dve.scalar_tensor_tensor(keep[:], side[:], 1.0 / SCALE, mask[:], ALU.mult, ALU.mult))
                    p_done(dve.tensor_scalar(pen[:], mask[:], -1.0, FAR, ALU.add, ALU.mult))
                    p_settle()
                    p_done(dve.tensor_tensor(kb[:], keep[:], pen[:], ALU.add))
                    p_settle()
                dve.sem_inc(s["bias_rows"], 1)
                p_done(dve.tensor_scalar(penc[:], maskc[:], -1.0, 3e38, ALU.add, ALU.mult))
                p_done(dve.scalar_tensor_tensor(keepc[:], kbc[:].bitcast(F32), -SCALE, sidec[:], ALU.mult, ALU.add))
                p_settle()
                p_done(dve.tensor_tensor(ebc[:], keepc[:], penc[:], ALU.add))
                p_settle()
                dve.wait_ge(s["ffn_w_in"], 16)
                fp6_scale(dve, p_done, p_settle, wfr[:].rearrange("p (n k) -> p n k", k=32), NB)
                fp6_round(dve, p_done, p_settle, NB, wdq[:].rearrange("p (n k) -> p n k", k=32), s["wd_quant"])
                dve.wait_ge(s["gates_done"], 1)
                dve.wait_ge(s["wd_quant"], 1)
                dve.wait_ge(s["w1_in"], 32)
                for half in range(2):
                    n = E * FB // 2
                    hi, lo = (t[:, n * half:n * half + n].rearrange("p n m -> p (n m)") for t in (w1h, w1l))
                    dve.tensor_copy(hi, w1_raw[half]).then_inc(s["w1_split"], 1)
                    dve.wait_ge(s["w1_split"], 2 * half + 1)
                    dve.tensor_tensor(lo, w1_raw[half], hi.bitcast(F32), ALU.subtract).then_inc(s["w1_split"], 1)

            def enter(b):
                done, settle, _ = counted(dve, s["next_step"], NEXT_STEPS * b)
                dve.wait_ge(s["x_in"], 16 * b + 16)
                spread(xin, "lnx", done, settle)
                center(xin, b, "lnx", xn[0], s["xn_sb"][0])
                keys_values(b, 0)
                queries(b, 0)
                dve.wait_ge(s["sel_in"], 16)
                dve.tensor_copy(rnd[:, NSEL // 2:], sel_raw[:, NSEL // 2:]).then_inc(s["rounded"], 1)
                for n in range(2):
                    max_unit(b, 0, n, n % 2)

            def body(b0, b1, m, nxt):
                def steps(gs):
                    for g in gs if m is not None else ():
                        step(m, g)

                none = (None,) * 3
                n_done, n_settle, n_n = counted(dve, s["next_step"], nxt * NEXT_STEPS) if nxt is not None else none
                a_done, a_settle, a_n = counted(dve, s["attn0_step"], b0 * ATTN0_STEPS) if b0 is not None else none
                y_done, y_settle, y_n = counted(dve, s["attn1_step"], b1 * ATTN1_STEPS) if b1 is not None else none
                z_done, z_settle, z_n = counted(dve, s["moe_step"], m * MOE_STEPS) if m is not None else none
                for n in range(8):
                    if b0 is not None and n >= 2:
                        max_unit(b0, 0, n, n % 2)
                    if m is not None:
                        if n == 2:
                            router(m, z_done, z_settle)
                        if n == 3:
                            router_weights(m, z_done, z_settle)
                    steps(S0_STEPS[n])
                if b1 is not None:
                    batch_bias(b1)
                    keys_values(b1, 1)
                steps(MID_STEPS[0])
                if b1 is not None:
                    queries(b1, 1)
                steps(MID_STEPS[1])
                steps(MID_STEPS[2])
                if b1 is not None:
                    stacks(b1, 1)
                steps(MID_STEPS[3])
                if first_of(b0):
                    prepare()
                if b1 is not None:
                    max_unit(b1, 1, 0, 0)
                steps(MID_STEPS[4])
                if b1 is not None:
                    max_unit(b1, 1, 1, pair_of(1, b0))
                for n in range(8):
                    if b1 is not None and n < 6:
                        max_unit(b1, 1, n + 2, pair_of(n, b0))
                    if nxt is not None and n == 3:
                        dve.wait_ge(s["x_in"], 16 * nxt + 16)
                        spread(xin, "lnx", n_done, n_settle)
                    if nxt is not None and n == 5:
                        center(xin, nxt, "lnx", xn[0], s["xn_sb"][0])
                    steps(X_STEPS[n])
                steps(X_STEPS[8])
                for n in range(8):
                    if n == 0 and b0 is not None:
                        wait_apart(dve, s["pvs_sb"], b0 + 1)
                        sums(pvs, a_done, a_settle)
                        normalize(0, pvs, a_settle)
                    if n == PROJECT_AT and b0 is not None:
                        dve.wait_ge(s["y_ps"][0], b0 + 1)
                        dve.scalar_tensor_tensor(x1[:], OP[:, S:2 * S].rearrange("p (q d) -> p q d", q=2), gate[:, 0:1],
                                                 xres[:], ALU.mult, ALU.add).then_inc(s["x1_sb"], 1)
                        dve.wait_ge(s["x1_sb"], b0 + 1)
                        spread(x1, "lnf", a_done, a_settle)
                        center(x1, b0, "lnf", xf, s["xf_sb"])
                        dve.wait_ge(s["xf_sb"], b0 + 1)
                        fp6_scale(dve, a_done, a_settle, xf[:].rearrange("p q (n k) -> p (q n) k", k=32), 2 * NB)
                        fp6_round(dve, a_done, a_settle, 2 * NB, xd[:], s["xd_sb"])
                    steps(A1_STEPS[n])
                if b1 is not None:
                    wait_apart(dve, s["pv_ps"][1], b1 + 1)
                    sums(PV, y_done, y_settle)
                for gs in TAIL_STEPS[0:3]:
                    steps(gs)
                if b1 is not None:
                    normalize(1, PV, y_settle)
                if nxt is not None:
                    keys_values(nxt, 0)
                steps(TAIL_STEPS[3])
                if nxt is not None:
                    queries(nxt, 0)
                steps(TAIL_STEPS[4])
                steps(TAIL_STEPS[5])
                if b1 is not None:
                    dve.wait_ge(s["y_ps"][1], b1 + 1)
                    if not first_of(b1):
                        dve.wait_ge(s["xb3_sb"], b1)
                    dve.scalar_tensor_tensor(x3[:], PV[:, 0:S].rearrange("p (q d) -> p q d", q=2), gate[:, 2:3],
                                             x2[:], ALU.mult, ALU.add).then_inc(s["x3_sb"], 1)
                    dve.wait_ge(s["x3_sb"], b1 + 1)
                if b0 is not None:
                    dve.wait_ge(s["ffn_ps"], b0 + 1)
                    dve.wait_ge(s["x1b_sb"], b0 + 1)
                    dve.scalar_tensor_tensor(x2[:], PV[:, S:2 * S].rearrange("p (q d) -> p q d", q=2), gate[:, 1:2],
                                             x1b[:], ALU.mult, ALU.add).then_inc(s["x2_sb"], 1)
                steps(TAIL_STEPS[6])
                if b1 is not None:
                    spread(x3, "lnz", y_done, y_settle)
                steps(TAIL_STEPS[7])
                if b0 is not None:
                    dve.wait_ge(s["x2_sb"], b0 + 1)
                    spread(x2, "lny", a_done, a_settle)
                if b1 is not None:
                    if not first_of(b1):
                        dve.wait_ge(s["x3T_ps"], b1)
                    center(x3, b1, "lnz", x3n, s["x3n_sb"])
                if b0 is not None:
                    center(x2, b0, "lny", xn[1], s["xn_sb"][1])
                steps(TAIL_STEPS[8])
                if nxt is not None:
                    max_unit(nxt, 0, 0, 0)
                if m is not None:
                    moe_spread(m, z_done, z_settle)
                if b1 is not None:
                    dve.wait_ge(s["x3h_sb"], b1 + 1)
                    dve.tensor_tensor(x3l[:], x3T[:], x3h[:].bitcast(F32), ALU.subtract).then_inc(s["x3l_sb"], 1)
                if nxt is not None:
                    max_unit(nxt, 0, 1, 1)
                if m is not None:
                    moe_center(m)
                for got, want in ((n_n, NEXT_STEPS), (a_n, ATTN0_STEPS), (y_n, ATTN1_STEPS), (z_n, MOE_STEPS)):
                    assert got is None or got[0] == want, (got, want)

            dve.sem_inc(s["zn_sb"], 1)
            dve.wait_ge(s["const_in"], 16)
            enter(0)
            stages(lambda b: None, body, dve.Fori)

        @block.gpsimd
        def _(pool):
            def root(name, k, mv_, ve, rs):
                wait_apart(pool, s[name + "_stats"], k)
                pool.tensor_scalar(ve[:].unsqueeze(2), mv_[:, :, 1:2], EPS, None, ALU.add).then_inc(s[name + "_veps"], 1)
                pool.wait_ge(s[name + "_veps"], k)
                pool.tensor_tensor(rs[:], ve[:], halfs[:], ALU.pow).then_inc(s[name + "_rstd"], 1)

            def ln(name, b):
                root(name, b + 1, mv[name], veps[name], rstd[name])

            def mask_unit(b, n):
                tp, kt, u = unit(n)
                wait_apart(pool, s["exp_sb"][0], 8 * b + n + 1)

                def keep(rows, q0, per_q, per_key, base):
                    blk = P[0:rows, kt, 2 * tp + u, :, q0:q0 + 64]
                    pool.affine_select(out=blk, in_=blk, pattern=[[0, 4], [per_q, 64]], compare_op=ALU.is_ge, fill=0.0,
                                       base=base, channel_multiplier=per_key).then_inc(s["p_masked"], 1)
                if kt == 0:
                    keep(128, 0, 0, -1, 63)
                    keep(128, 64, 0, 1, -64)
                else:
                    keep(128, 192, 0, 1, -64)
                    keep(64, 128, 1, -1, 0)

            def step(m, g):
                if g % 4 == 3 and g >= 7:
                    e = g // 4 - 1
                    pool.wait_ge(s["te_sb"], E * m + e + 1)
                    if e == 0:
                        pool.wait_ge(s["x3T_sb"], m + 1)
                    else:
                        pool.wait_ge(s["acc_sb"], E * m + e)
                    pool.tensor_tensor(acc[:], x3T[:] if e == 0 else acc[:], te[:, e % 2], ALU.add).then_inc(s["acc_sb"], 1)

            def body(b0, b1, m, nxt):
                def steps(gs):
                    for g in gs if m is not None else ():
                        step(m, g)

                if m is not None:
                    pool.wait_ge(s["x3_sb"], m + 1)
                    pool.wait_ge(s["out_sb"], m + 1)
                    pool.tensor_tensor(xb3[:], x3[:], gbet[:].unsqueeze(1).to_broadcast([128, 2, D]), ALU.add)\
                        .then_inc(s["xb3_sb"], 1)
                for gs in S0_STEPS + MID_STEPS:
                    steps(gs)
                for n in range(8):
                    if nxt is not None and n == 4:
                        ln("lnx", nxt)
                    if b0 is not None:
                        mask_unit(b0, n)
                    steps(X_STEPS[n])
                steps(X_STEPS[8])
                for n in range(8):
                    if n == PROJECT_AT and b0 is not None:
                        pool.wait_ge(s["x1_sb"], b0 + 1)
                        ln("lnf", b0)
                        pool.tensor_tensor(x1b[:], x1[:], gfb[:].unsqueeze(1).to_broadcast([128, 2, D]), ALU.add)\
                            .then_inc(s["x1b_sb"], 1)
                    steps(A1_STEPS[n])
                for gs in TAIL_STEPS[0:7]:
                    steps(gs)
                if b1 is not None:
                    ln("lnz", b1)
                steps(TAIL_STEPS[7])
                if b0 is not None:
                    ln("lny", b0)
                steps(TAIL_STEPS[8])
                if m is not None:
                    root("z", m + 1, zmv, zve, zrs)
                    pool.wait_ge(s["zn_sb"], m + 2)
                    pool.tensor_tensor(zg[:], zn[:], ggam[:].unsqueeze(1).to_broadcast([128, 2, D]), ALU.mult)\
                        .then_inc(s["zg_sb"], 1)
                    pool.wait_ge(s["zg_sb"], m + 1)
                    pool.wait_ge(s["stored"], 16 * m + 16)
                    pool.tensor_tensor(outt[:], zg[:], xb3[:], ALU.add).then_inc(s["out_sb"], 1)

            pool.memset(halfs[:], -0.5).then_inc(s["pool_prep"], 1)
            for l in range(2):
                pool.memset(vst[l][:], 0.0).then_inc(s["pool_prep"], 1)
            pool.wait_ge(s["pool_prep"], 3)
            ln("lnx", 0)
            for l in range(2):
                pool.memset(vst[l][:, :, 0:8, 16:24], 1.0).then_inc(s["ones_set"], 1)
                pool.memset(vst[l][:, :, 8:16, 24:32], 1.0).then_inc(s["ones_set"], 1)
            pool.memset(outt[:], 0.0).then_inc(s["out_sb"], 1)
            pool.wait_ge(s["gates_done"], 1)
            for src, dst, g in (("ffn_b", gfb, 1), ("gamma", ggam, 3), ("beta", gbet, 3)):
                pool.tensor_scalar(dst[:], c(src), gate[:, g:g + 1], None, ALU.mult).then_inc(s["pool_prep"], 1)
            pool.wait_ge(s["pool_prep"], 6)
            stages(lambda b: None, body, pool.Fori)


ORDER = np.concatenate([np.arange(0, 128), np.arange(192, 256), np.arange(128, 192)])


def head_of(tile, j, slot_):
    i, t = 2 * slot_ + j // 2, 2 * tile + j % 2
    return 4 * i + t


def tokens(a):
    return np.ascontiguousarray(a[:, ORDER].reshape(B, 2, 128, D).transpose(2, 0, 1, 3))


def constants(v):
    cst, selectors = np.zeros((128, NCONST), np.float32), np.zeros((128, NSEL), np.float32)

    def put(name, a):
        dst, (lo, hi) = (cst, CONST_AT[name]) if name in CONST_AT else (selectors, SEL_AT[name])
        a = np.asarray(a, np.float32)
        dst[0:a.shape[0], lo:hi] = a.reshape(a.shape[0], hi - lo)
    put("ident", np.eye(128))
    put("eye", np.eye(128))
    sel = np.zeros((128, 4, 4, 128), np.float32)
    for t in range(4):
        for i in range(4):
            for d in range(HD):
                ch, row = HD * (4 * i + t) + d, 32 * i + d
                for kind, rows in ((0, (0, 16)), (1, (8,)), (2, (0, 8)), (3, (16,))):
                    for r in rows:
                        sel[ch, kind, t, row + r] = 1
    put("sel", sel)
    aux = np.zeros((1, 128))
    aux[0, ROW_BIAS::32] = 1
    put("auxsel", aux)
    causal = np.zeros((128, 64))
    causal[0:64] = np.where(np.arange(64)[None] > np.arange(64)[:, None], -FAR, 0)
    put("causal", causal)
    wsel = np.zeros((2 * E, E, 128))
    for e in range(E):
        wsel[e, e] = wsel[E + e, e] = 1
    put("wsel", wsel)
    qaux, kaux = np.zeros((128, 1)), np.zeros((128, 1))
    qaux[ROW_BIAS::32] = 1
    kaux[ROW_MAX::32] = 1
    put("qaux", qaux)
    put("kaux", kaux)
    put("iota", np.tile(np.arange(E), (128, 1)))
    put("b1", v["L1_ffn_b1"].reshape(E * FB, 128).T)
    put("b2", v["L1_ffn_b2"].T)
    put("bq", np.stack([v["L0_xattn_bq"], v["L1_xattn_Wq_b"]], 1))
    put("bk", np.stack([v["L0_xattn_bk"], v["L1_xattn_Wkv_b"][0:D]], 1))
    g = [v["g_xattn"][0], v["g_ffn"][0], v["g_xattn"][1], v["g_ffn"][1]]
    for name, row in (("gates", g), ("bv", np.concatenate([v["L0_xattn_bv"], v["L1_xattn_Wkv_b"][D:]])),
                      ("ffn_b", v["L0_ffn_bias"]), ("gamma", v["L1_ffn_gamma"]), ("beta", v["L1_ffn_beta"]),
                      ("br", v["L1_ffn_br"])):
        put(name, np.broadcast_to(np.asarray(row)[None], (128, len(row))))
    return cst, selectors


def out_weight(w, b):
    o = np.zeros((128, 2, D), np.float32)
    for tile in range(2):
        for j in range(4):
            for slot_ in range(2):
                h, r = head_of(tile, j, slot_), 32 * j + 8 * slot_
                o[r:r + HD, tile] = w[HD * h:HD * h + HD]
    o[16, 0] = b
    return o


def kernel(**inputs):
    import concourse.bacc as bacc
    from concourse.bass_utils import run_bass_kernel_spmd

    v = {k: np.asarray(a) for k, a in inputs.items()}
    side, mask = v["fside_BxS2_0"][:, ORDER], v["mask_BxS2_bk0"][:, ORDER]
    wkv = v["L1_xattn_Wkv_w"]
    w_attn = np.zeros((128, 2, 5, D), np.float32)
    w_attn[:, 0, 0], w_attn[:, 0, 1], w_attn[:, 0, 2] = v["L0_xattn_Wq"], v["L0_xattn_Wk"], v["L0_xattn_Wv"]
    w_attn[:, 1, 0], w_attn[:, 1, 1], w_attn[:, 1, 2] = v["L1_xattn_Wq_w"].T, wkv[0:D].T, wkv[D:].T
    w_attn[:, 0, 3:] = out_weight(v["L0_xattn_Wo"], v["L0_xattn_bo"])
    w_attn[:, 1, 3:] = out_weight(v["L1_xattn_out_w"].T, v["L1_xattn_out_b"])
    cst, selectors = constants(v)
    arrays = {
        "x": tokens(v["x"]), "ctx": tokens(v["ctx_1024"]),
        "side_col": side.reshape(B, 2, 128).transpose(2, 0, 1), "mask_col": mask.reshape(B, 2, 128).transpose(2, 0, 1),
        "side_row": side, "mask_row": mask, "const": cst, "selectors": selectors,
        "w_attn": w_attn, "w_ffn": v["L0_ffn_weight"], "w_router": v["L1_ffn_Wr"].T,
        "w1": v["L1_ffn_W1"].reshape(E * FB, 128, D).transpose(2, 0, 1),
        "w2": v["L1_ffn_W2"].reshape(E, D, FB, 128).transpose(3, 0, 2, 1).reshape(128, E * FB, D),
    }
    arrays = {f"in_{k}": np.ascontiguousarray(a) for k, a in arrays.items()}
    nc = bacc.Bacc("TRN2", target_bir_lowering=False, num_devices=1)
    args = [nc.dram_tensor(k, a.shape, mybir.dt.from_np(a.dtype), kind="ExternalInput").ap() for k, a in arrays.items()]
    args.append(nc.dram_tensor("out_0", (128, B, 2, D), F32, kind="ExternalOutput").ap())
    program(nc, *args)
    got = run_bass_kernel_spmd(nc, [arrays], core_ids=[0]).results[0]["out_0"]
    back = np.argsort(ORDER)
    return np.ascontiguousarray(got.transpose(1, 2, 0, 3).reshape(B, S, D)[:, back])
```
